# Optimizing a Trainium2 kernel written in Bass

```python
import numpy as np
import jax
import jax.numpy as jnp

def _softmax(x, axis=-1):
    return jax.nn.softmax(x, axis=axis)

def _gelu(x):
    return jax.nn.gelu(x, approximate=True)

def _silu(x):
    return jax.nn.silu(x)

def _sigmoid(x):
    return jax.nn.sigmoid(x)

def _layernorm(x, axis=-1, eps=1e-05):
    m = jnp.mean(x, axis=axis, keepdims=True)
    v = jnp.var(x, axis=axis, keepdims=True)
    return (x - m) / jnp.sqrt(v + eps)

def _scatter_add(tgt, idx, src, axis=0):
    return tgt.at[idx].add(src)

def _segment_sum(src, seg, n):
    return jax.ops.segment_sum(src, seg, n)
kernel_name = 'mk_cond_resid_d4_seqx_r4_a2c222'

def setup_inputs(seed: int=0):
    np.random.seed(seed)
    _w = jnp.asarray

    def _rec_inputs():
        import jax
        import jax.numpy as jnp
        _rk = jax.random.key(seed)
        x = -0.000125 + 0.9999 * jax.random.normal(jax.random.fold_in(_rk, 1), (8, 512, 256), jnp.float32)
        _lenS = 512 - jax.random.randint(jax.random.fold_in(_rk, 7), (8,), 0, max(1, 512 // 4) + 1, jnp.int32)
        _lenS2 = 512 - jax.random.randint(jax.random.fold_in(_rk, 8), (8,), 0, max(1, 512 // 4) + 1, jnp.int32)
        cond_1024 = 0.00782532 + 1.00527 * jax.random.normal(jax.random.fold_in(_rk, 11), (8, 256), jnp.float32)
        return (x, cond_1024)
    x, cond_1024 = _rec_inputs()

    def _L0_cond_setup():
        import jax, jax.numpy as jnp
        import numpy as np
        INV_SQRT2 = 0.7071067811865476
        key = jax.random.key(seed)
        k1, k2, k3, k4 = jax.random.split(key, 4)
        B, N, d = (8, 1024, 256)
        scale = 1.0 / np.sqrt(d)
        return {'v': jax.random.normal(k1, (B, N, d), dtype=jnp.float32), 'q_pool': jax.random.normal(k2, (B, d), dtype=jnp.float32), 'W1': jax.random.normal(k3, (d, d), dtype=jnp.float32) * scale, 'b1': jnp.zeros((d,), dtype=jnp.float32), 'W2': jax.random.normal(k4, (d, d), dtype=jnp.float32) * scale, 'b2': jnp.zeros((d,), dtype=jnp.float32)}
    _L0_cond_all = _L0_cond_setup()
    _L0_cond_in = {k: v for k, v in _L0_cond_all.items() if k in ('W1', 'b1', 'W2', 'b2')}
    del _L0_cond_all

    def _L1_cond_setup():
        import jax, jax.numpy as jnp
        import numpy as np
        D, HS, HE, E, K = (256, 512, 256, 8, 2)
        B, T = (4, 256)
        N_SHARED = 1
        key = jax.random.key(seed)
        ks = jax.random.split(key, 9)
        g = lambda k, shape, s: jax.random.normal(k, shape, jnp.float32) * s
        return {'x': g(ks[0], (B, T, D), 1.0), 't_emb': g(ks[1], (B, D), 1.0), 'router_W': g(ks[2], (2 * D, E), 0.01), 'router_bias': jnp.zeros((E,), jnp.float32), 'w1': g(ks[3], (D, HS), 0.02), 'w3': g(ks[4], (D, HS), 0.02), 'w2': g(ks[5], (HS, D), 0.02), 'W1e': g(ks[6], (E, D, HE), 0.02), 'W2e': g(ks[7], (E, HE, D), 0.02)}
    _L1_cond_all = _L1_cond_setup()
    _L1_cond_in = {k: v for k, v in _L1_cond_all.items() if k in ('router_W', 'router_bias', 'w1', 'w3', 'w2', 'W1e', 'W2e')}
    del _L1_cond_all

    def _L2_cond_setup():
        import jax, jax.numpy as jnp
        import numpy as np
        N, T, D, H = (64, 128, 256, 256)
        key = jax.random.key(seed)
        k1, k2, k3, k4 = jax.random.split(key, 4)
        x = jax.random.normal(k1, (N, T, D), dtype=jnp.float32)
        h0 = jax.random.normal(k2, (N, H), dtype=jnp.float32)
        Wx = jax.random.normal(k3, (D, 4 * H), dtype=jnp.float32) / np.sqrt(D)
        Wh = jax.random.normal(k4, (H, 4 * H), dtype=jnp.float32) / np.sqrt(H)
        b = jnp.zeros((4 * H,), dtype=jnp.float32)
        return {'x': x, 'h0': h0, 'Wx': Wx, 'Wh': Wh, 'b': b}
    _L2_cond_all = _L2_cond_setup()
    _L2_cond_in = {k: v for k, v in _L2_cond_all.items() if k in ('Wx', 'Wh', 'b')}
    del _L2_cond_all

    def _L3_cond_setup():
        import jax, jax.numpy as jnp
        import numpy as np
        LATENT = 256
        key = jax.random.key(seed)
        k1, k2, k3, k4 = jax.random.split(key, 4)
        B, T, D = (64, 128, LATENT)
        h_t = jax.random.normal(k1, (B, D), dtype=jnp.float32)
        z = jax.random.normal(k2, (B, T, D), dtype=jnp.float32)
        bound = 1.0 / np.sqrt(2 * D)
        W = jax.random.uniform(k3, (D, 2 * D), minval=-bound, maxval=bound, dtype=jnp.float32)
        b = jax.random.uniform(k4, (D,), minval=-bound, maxval=bound, dtype=jnp.float32)
        alpha = jnp.full((D,), 0.1, dtype=jnp.float32)
        return {'h_t': h_t, 'z': z, 'W': W, 'b': b, 'alpha': alpha}
    _L3_cond_all = _L3_cond_setup()
    _L3_cond_in = {k: v for k, v in _L3_cond_all.items() if k in ('W', 'b', 'alpha')}
    del _L3_cond_all
    return {'x': x, 'cond_1024': cond_1024, 'L0_cond_W1': _L0_cond_in['W1'], 'L0_cond_b1': _L0_cond_in['b1'], 'L0_cond_W2': _L0_cond_in['W2'], 'L0_cond_b2': _L0_cond_in['b2'], 'L1_cond_router_W': _L1_cond_in['router_W'], 'L1_cond_router_bias': _L1_cond_in['router_bias'], 'L1_cond_w1': _L1_cond_in['w1'], 'L1_cond_w3': _L1_cond_in['w3'], 'L1_cond_w2': _L1_cond_in['w2'], 'L1_cond_W1e': _L1_cond_in['W1e'], 'L1_cond_W2e': _L1_cond_in['W2e'], 'L2_cond_Wx': _L2_cond_in['Wx'], 'L2_cond_Wh': _L2_cond_in['Wh'], 'L2_cond_b': _L2_cond_in['b'], 'L3_cond_W': _L3_cond_in['W'], 'L3_cond_b': _L3_cond_in['b'], 'L3_cond_alpha': _L3_cond_in['alpha']}

def reference(x, cond_1024, L0_cond_W1, L0_cond_b1, L0_cond_W2, L0_cond_b2, L1_cond_router_W, L1_cond_router_bias, L1_cond_w1, L1_cond_w3, L1_cond_w2, L1_cond_W1e, L1_cond_W2e, L2_cond_Wx, L2_cond_Wh, L2_cond_b, L3_cond_W, L3_cond_b, L3_cond_alpha):
    import jax
    import jax.numpy as jnp

    def _L0_cond_ref(v, q_pool, W1, b1, W2, b2):
        import jax, jax.numpy as jnp
        import numpy as np
        INV_SQRT2 = 0.7071067811865476
        B, N, d = v.shape
        h = jax.nn.silu(q_pool @ W1.T + b1)
        gate = jax.nn.sigmoid(h @ W2.T + b2)[:, None, :]
        levels = int(np.log2(N))
        a = v
        details = []
        for _ in range(levels):
            e, o = (a[:, 0::2], a[:, 1::2])
            details.append((e - o) * INV_SQRT2)
            a = (e + o) * INV_SQRT2
        a = a * gate
        for dc in reversed(details):
            dc = dc * gate
            e = (a + dc) * INV_SQRT2
            o = (a - dc) * INV_SQRT2
            n = e.shape[1]
            a = jnp.stack([e, o], axis=2).reshape(B, 2 * n, d)
        return v + a

    def _L1_cond_ref(x, t_emb, router_W, router_bias, w1, w3, w2, W1e, W2e):
        import jax, jax.numpy as jnp
        import numpy as np
        D, HS, HE, E, K = (256, 512, 256, 8, 2)
        B, T = (4, 256)
        N_SHARED = 1
        Bb, Tt, C = x.shape
        xf = x.reshape(-1, C)
        tf = jnp.broadcast_to(t_emb[:, None, :], (Bb, Tt, C)).reshape(-1, C)
        N = xf.shape[0]
        shared = jax.nn.silu(xf @ w1) * (xf @ w3) @ w2
        s = jax.nn.sigmoid((jnp.concatenate([xf, tf], axis=-1) @ router_W).astype(jnp.float32))
        sel_scores = s + router_bias
        _, topk_idx = jax.lax.top_k(sel_scores, K)
        s_sel = jnp.take_along_axis(s, topk_idx, axis=1)
        denom = s_sel.sum(axis=1, keepdims=True)
        gates = jnp.where(denom > 1e-09, s_sel / (denom + 1e-09), 1.0 / K).astype(x.dtype)
        combine = jnp.zeros((N, E), x.dtype).at[jnp.arange(N)[:, None], topk_idx].add(gates)
        h = jax.nn.gelu(jnp.einsum('nc,ech->enh', xf, W1e), approximate=False)
        y = jnp.einsum('enh,ehc->enc', h, W2e)
        routed = jnp.einsum('ne,enc->nc', combine, y)
        return ((shared + routed) / (N_SHARED + K)).reshape(Bb, Tt, C)

    def _L2_cond_ref(x, h0, Wx, Wh, b):
        import jax, jax.numpy as jnp
        import numpy as np
        N, T, D, H = (64, 128, 256, 256)
        Hdim = h0.shape[1]
        xW = jnp.einsum('ntd,dg->ntg', x, Wx) + b
        c0 = jnp.zeros_like(h0)

        def step(carry, xw_t):
            prev_h, prev_c = carry
            A = xw_t + prev_h @ Wh
            i = jax.nn.sigmoid(A[:, 0:Hdim])
            f = jax.nn.sigmoid(A[:, Hdim:2 * Hdim])
            o = jax.nn.sigmoid(A[:, 2 * Hdim:3 * Hdim])
            g = jnp.tanh(A[:, 3 * Hdim:4 * Hdim])
            next_c = f * prev_c + i * g
            next_h = o * jnp.tanh(next_c)
            return ((next_h, next_c), next_h)
        _, hs = jax.lax.scan(step, (h0, c0), jnp.swapaxes(xW, 0, 1))
        return jnp.swapaxes(hs, 0, 1)

    def _L3_cond_ref(h_t, z, W, b, alpha):
        import jax, jax.numpy as jnp
        import numpy as np
        LATENT = 256
        D = h_t.shape[-1]
        Wh = W[:, :D]
        Wz = W[:, D:]
        leak = 1.0 - alpha

        def step(h, z_t):
            gate = jax.nn.sigmoid(h @ Wh.T + z_t @ Wz.T + b)
            h_new = jnp.tanh(h * leak + gate * z_t)
            return (h_new, h_new)
        _, hs = jax.lax.scan(step, h_t, jnp.swapaxes(z, 0, 1))
        return jnp.swapaxes(hs, 0, 1)
    x = x + _L0_cond_ref(x, cond_1024, L0_cond_W1, L0_cond_b1, L0_cond_W2, L0_cond_b2)
    x = x + _L1_cond_ref(x, cond_1024, L1_cond_router_W, L1_cond_router_bias, L1_cond_w1, L1_cond_w3, L1_cond_w2, L1_cond_W1e, L1_cond_W2e)
    x = x + _L2_cond_ref(x, cond_1024, L2_cond_Wx, L2_cond_Wh, L2_cond_b)
    x = x + _L3_cond_ref(cond_1024, x, L3_cond_W, L3_cond_b, L3_cond_alpha)
    return x

_drawn_inputs = setup_inputs


def setup_inputs(seed=0):
    import zlib

    import numpy as np

    out = dict(_drawn_inputs(seed))
    spreads = {'L0_cond_b1': (0.0, 0.8),
     'L0_cond_b2': (0.0, 0.8),
     'L1_cond_router_bias': (0.0, 0.526),
     'L2_cond_b': (0.0, 0.701),
     'L3_cond_alpha': (0.10000000149011612, 0.6)}
    factors = {'L1_cond_router_W': 4.998, 'L1_cond_W1e': 3.916, 'L1_cond_W2e': 3.523, 'L3_cond_b': 36.569}
    for name, (base, spread) in spreads.items():
        noise = np.random.default_rng([zlib.crc32(name.encode()), seed]).standard_normal(out[name].shape)
        drawn = base * np.exp(spread * noise) if base else spread * noise
        out[name] = jnp.asarray(drawn.astype(out[name].dtype))
    for name, factor in factors.items():
        out[name] = (out[name] * factor).astype(out[name].dtype)
    return out
```

```python
from contextlib import ExitStack

import numpy as np
import concourse.bass as bass
from concourse import mybir

F32, F16, BF16, U32 = mybir.dt.float32, mybir.dt.float16, mybir.dt.bfloat16, mybir.dt.uint32
ALU = mybir.AluOpType
ACT = mybir.ActivationFunctionType

B, T, D = 8, 512, 256
P = 128
KD = D // P
STEPS = 16
TOK = STEPS * B
CHUNKS = T // STEPS
HS, HE, E = 512, 256, 8
GATES = 4 * KD
SCALE = 256.0

SHARED = 2
UNITS = SHARED + E
PIECES = [("up", q, n) for q in range(SHARED) for n in range(4)]
for q in range(UNITS):
    if q == UNITS - 1:
        PIECES += [None]
    PIECES += [("down", q, n) for n in range(2)]
    if q + 2 < UNITS:
        PIECES += [("up", q + 2, n) for n in range(2)]


def last_piece(kind, q):
    return max(n for n, p in enumerate(PIECES) if p and p[:2] == (kind, q))


ACT_AT, GLU_AT, SUM_AT = [], [], []
for q in range(UNITS):
    at, place = 1 + last_piece("up", q) // 3, last_piece("up", q) % 3
    ACT_AT.append((at, 1) if place == 0 else (at + 1, 0))
    GLU_AT.append((at + 1, 0) if place == 0 else (at + 1, 1))
    at, place = 1 + last_piece("down", q) // 3, last_piece("down", q) % 3
    SUM_AT.append((at, 1) if place == 0 else (at + 1, 0))


class Chunk:

    def __init__(self, i, c):
        self.i, self.c = i, c

    def __add__(self, n):
        return Chunk(self.i, self.c + n)

    @property
    def ring(self):
        return self.c % 2

    def count(self, per_chunk, more=0):
        n = self.c * per_chunk + more
        return n if self.i is None else self.i * (2 * per_chunk) + n

    def pairs(self, per_pair, more=0):
        n = self.c // 2 * per_pair + more
        return n if self.i is None else self.i * per_pair + n

    def real(self):
        return self.i is not None or 0 <= self.c < CHUNKS


def wait(eng, sem, count):
    if not isinstance(count, int) or count > 0:
        eng.wait_ge(sem, count)


def rounds(eng, round_):
    for k in range(-2, 2):
        round_(Chunk(None, k))
    with eng.Fori(0, (CHUNKS - 4) // 2) as i:
        round_(Chunk(i, 2))
        round_(Chunk(i, 3))
    for k in range(CHUNKS - 2, CHUNKS + 2):
        round_(Chunk(None, k))


def build(nc, x, cond, L0_W1, L0_b1, L0_W2, L0_b2, router_W, router_b, w1, w3, w2, W1e, W2e,
          Wx, Wh, lstm_b, L3_W, L3_b, L3_alpha, out):
    with ExitStack() as ctx:
        def sb(name, shape, dt=F32):
            return ctx.enter_context(nc.sbuf_tensor(name, shape, dt))

        def pb(name, shape):
            return ctx.enter_context(nc.psum_tensor(name, shape, F32))

        def sem(name):
            return ctx.enter_context(nc.semaphore(name))

        ident = sb("ident", [P, P])
        expert_row = sb("expert_row", [P, E])
        euler = sb("euler", [P, E])
        ones = sb("ones", [P, P], BF16)
        gateW1 = sb("gateW1", [P, KD, D])
        gateW2 = sb("gateW2", [P, KD, D])
        gateW1T = sb("gateW1T", [P, KD, D])
        gateW2T = sb("gateW2T", [P, KD, D])
        vec_rows = sb("vec_rows", [3 * KD, P])
        vecs = sb("vecs", [P, 3 * KD])
        routerW = sb("routerW", [P, 2 * KD, E])
        router_bias = sb("router_bias", [P, E])
        w1_sb = sb("w1_sb", [P, KD, HS])
        w3_sb = sb("w3_sb", [P, KD, HS])
        w2_sb = sb("w2_sb", [P, HS // P, D])
        W1e_sb = sb("W1e_sb", [P, E, KD, HE])
        W2e_sb = sb("W2e_sb", [P, E, HE // P, D])
        Wx_sb = sb("Wx_sb", [P, KD, 4 * D])
        Wh_sb = sb("Wh_sb", [P, KD, 4 * D])
        Wh_hi = sb("Wh_hi", [P, KD, 4 * D], F16)
        Wh_lo = sb("Wh_lo", [P, KD, 4 * D], F16)
        leakW = sb("leakW", [P, KD, 2 * D])
        Wz = sb("Wz", [P, KD, D])
        Ws = sb("Ws", [P, KD, D])
        Ws_hi = sb("Ws_hi", [P, KD, D], F16)
        Ws_lo = sb("Ws_lo", [P, KD, D], F16)
        keep = sb("keep", [P, KD])
        leak = sb("leak", [P, KD, B])
        NB = 4 * D + D
        bias_row = sb("bias_row", [P, NB])
        bias_1 = sb("bias_1", [P, NB], BF16)
        bias_r1 = sb("bias_r1", [P, NB])
        bias_2 = sb("bias_2", [P, NB], BF16)
        bias_r2 = sb("bias_r2", [P, NB])
        bias_parts = sb("bias_parts", [P, NB], BF16)
        cond_sb = sb("cond_sb", [B, D])
        condT = sb("condT", [P, KD, B])
        cond2 = sb("cond2", [P, KD, B])
        cond_tok = sb("cond_tok", [P, KD, STEPS, B])
        pre = sb("pre", [P, 4, KD, B])
        sig = sb("sig", [P, 2, KD, B])
        hid_gate = sb("hid_gate", [P, KD, B])
        two_plus_gate = sb("two_plus_gate", [P, KD, B])
        cond_logits = sb("cond_logits", [P, E])
        x_in = sb("x_in", [P, 2, D])
        x1T = sb("x1T", [P, 2, KD, TOK])
        x2T = sb("x2T", [P, 2, KD, TOK])
        gate_tanh = sb("gate_tanh", [P, 2, 2 * TOK])
        glu_tmp = sb("glu_tmp", [P, 2 * TOK])
        hid = sb("hid", [P, 2, 2, TOK])
        moe_sum = sb("moe_sum", [P, D])
        neg_logits = sb("neg_logits", [P, E])
        exp_neg = sb("exp_neg", [P, E])
        exp_plus = sb("exp_plus", [P, E])
        scores = sb("scores", [P, E])
        biased = sb("biased", [P, E])
        best = sb("best", [P, E])
        took_wait = sb("took_wait", [P, 1])
        best_at = sb("best_at", [P, E], U32)
        best_atf = sb("best_atf", [P, 2])
        is_first = sb("is_first", [P, E])
        chosen = sb("chosen", [P, E])
        chosen_scores = sb("chosen_scores", [P, E])
        denom = sb("denom", [P, 1])
        denom_eps = sb("denom_eps", [P, 1])
        recip = sb("recip", [P, 1])
        norm = sb("norm", [P, 1])
        even = sb("even", [P, 1])
        normed = sb("normed", [P, E])
        evened = sb("evened", [P, E])
        combine = sb("combine", [P, 2, E])
        HB = KD * B
        cell_gates = sb("cell_gates", [P, 2, 5 * HB])
        parts = sb("parts", [P, 2 * HB])
        tanh_c = sb("tanh_c", [P, HB])
        h_hi = sb("h_hi", [P, 2, KD, B], F16)
        h_lo = sb("h_lo", [P, 2, KD, B], F16)
        h2 = sb("h2", [P, 2, KD, STEPS, B])
        z = sb("z", [P, 2, KD, STEPS, B])
        s_gate = sb("s_gate", [P, KD, B])
        gated = sb("gated", [P, KD, B])
        leaked = sb("leaked", [P, KD, B])
        s_pre = sb("s_pre", [P, KD, B])
        s_hi = sb("s_hi", [P, 2, KD, B], F16)
        s_lo = sb("s_lo", [P, 2, KD, B], F16)
        s_hist = sb("s_hist", [P, 2, KD, STEPS, B])
        y = sb("y", [P, KD, B, STEPS])
        y_out = sb("y_out", [P, 2, D])

        gates_ps = [pb(f"gates_ps{r}", [P, GATES, TOK]) for r in range(2)]
        up_ps = [pb(f"up_ps{r}", [P, 4, TOK]) for r in range(2)]
        tok_ps = pb("tok_ps", [P, 512])
        scan_ps = pb("scan_ps", [P, 4, TOK])

        w_gate, w_moe, w_lstm = sem("w_gate"), sem("w_moe"), sem("w_lstm")
        x_here = [sem("x_here0"), sem("x_here1")]
        y_stored = [sem("y_stored0"), sem("y_stored1")]
        consts = sem("consts")
        chain = sem("chain")
        ps_ready = sem("ps_ready")
        act_ready = sem("act_ready")
        gate_chain = sem("gate_chain")
        lstm_w_ready = sem("lstm_w_ready")
        x_turned, x1_ready = sem("x_turned"), sem("x1_ready")
        router_done, logits_ready, exp_ready = sem("router_done"), sem("logits_ready"), sem("exp_ready")
        route = sem("route")
        up_done = sem("up_done")
        tanh_ready, glu_half, glu_done = sem("tanh_ready"), sem("glu_half"), sem("glu_done")
        gelu_done = sem("gelu_done")
        down_done, sum_done = sem("down_done"), sem("sum_done")
        sum_turned, x2_ready = sem("sum_turned"), sem("x2_ready")
        gates_done, gates_act = sem("gates_done"), sem("gates_act")
        parts_done, cell_done, tanh_done = sem("parts_done"), sem("cell_done"), sem("tanh_done")
        hi_ready, lo_ready = sem("hi_ready"), sem("lo_ready")
        h2_ready = sem("h2_ready")
        z_ready = sem("z_ready")
        s_done, s_sig, s_gated, s_pre_done = sem("s_done"), sem("s_sig"), sem("s_gated"), sem("s_pre_done")
        s_hi_ready, s_lo_ready, leaked_ready = sem("s_hi_ready"), sem("s_lo_ready"), sem("leaked_ready")
        s_hist_ready = sem("s_hist_ready")
        y_ready, y_turned, y_out_ready = sem("y_ready"), sem("y_turned"), sem("y_out_ready")

        W_GATE, W_MOE, W_LSTM = 16 * 8, 16 * 5, 16 * 9
        ROUTE = 14

        def wait_hid(eng, c, q):
            if q < SHARED:
                wait(eng, glu_done, c.count(SHARED, q + 1))
            else:
                wait(eng, gelu_done, c.count(E, q - SHARED + 1))

        block = ctx.enter_context(nc.Block())

        @block.sync
        def _(sp):
            def load(dst, src, s):
                sp.dma_start(dst, src).then_inc(s, 16)

            def load_x(c):
                wait(sp, x_turned, c.count(1, -1))
                src = x[:, bass.ds(c.count(STEPS), STEPS), :]
                sp.dma_start(x_in[:, c.ring, :], src).then_inc(x_here[c.ring], 16)

            load(cond_sb[:, :], cond, w_gate)
            load(gateW1[:, :, :], L0_W1.rearrange("(o p) i -> p o i", p=P), w_gate)
            load(gateW2[:, :, :], L0_W2.rearrange("(o p) i -> p o i", p=P), w_gate)
            load_x(Chunk(None, 0))
            load(w1_sb[:, :, :], w1.rearrange("(k p) n -> p k n", p=P), w_moe)
            load(w3_sb[:, :, :], w3.rearrange("(k p) n -> p k n", p=P), w_moe)
            load(w2_sb[:, :, :], w2.rearrange("(k p) n -> p k n", p=P), w_moe)
            load(W1e_sb[:, :, :, :].rearrange("p e k n -> p (e k) n"),
                 W1e.rearrange("e (k p) n -> p (e k) n", p=P), w_moe)
            load(W2e_sb[:, :, :, :].rearrange("p e k n -> p (e k) n"),
                 W2e.rearrange("e (k p) n -> p (e k) n", p=P), w_moe)
            load_x(Chunk(None, 1))
            load(leakW[:, :, :], L3_W.rearrange("(o p) i -> p o i", p=P), w_lstm)
            load(Wx_sb[:, :, :], Wx.rearrange("(k p) n -> p k n", p=P), w_lstm)
            load(Wh_sb[:, :, :], Wh.rearrange("(k p) n -> p k n", p=P), w_lstm)

            def round_(k):
                if k.i is not None or k.c >= 0:
                    if (k + 2).real():
                        load_x(k + 2)
                done = k + -2
                if done.real():
                    wait(sp, y_out_ready, done.count(1, 1))
                    dst = out[:, bass.ds(done.count(STEPS), STEPS), :]
                    sp.dma_start(dst, y_out[:, done.ring, :]).then_inc(y_stored[done.ring], 16)

            rounds(sp, round_)
            for r in range(2):
                sp.wait_ge(y_stored[r], 16 * CHUNKS // 2)

        @block.gpsimd
        def _(pool):
            pool.memset(ident[:, :], 0.0).then_inc(consts, 1)
            pool.wait_ge(consts, 1)
            pool.affine_select(out=ident[:, :], in_=ident[:, :], compare_op=ALU.not_equal, fill=1.0,
                               base=0, pattern=[[-1, P]], channel_multiplier=1).then_inc(consts, 1)
            pool.iota(expert_row[:, :], pattern=[[1, E]], base=0, channel_multiplier=0,
                      allow_small_or_imprecise_dtypes=True).then_inc(consts, 1)
            pool.memset(ones[:, :], 1.0).then_inc(consts, 1)
            pool.memset(euler[:, :], float(np.e)).then_inc(consts, 1)
            pool.memset(bias_parts[:, :], 0.0).then_inc(consts, 1)
            pool.memset(cell_gates[:, 0, 4 * HB:5 * HB], 0.0).then_inc(consts, 1)
            pool.wait_ge(chain, CH_STATE)
            pool.wait_ge(hi_ready, 1)
            pool.wait_ge(s_hi_ready, 1)
            pool.tensor_tensor(h_lo[:, 0], cond2[:, :, :], h_hi[:, 0], ALU.subtract).then_inc(lo_ready, 1)
            pool.tensor_tensor(s_lo[:, 0], condT[:, :, :], s_hi[:, 0], ALU.subtract).then_inc(s_lo_ready, 1)
            pool.tensor_tensor(leaked[:, :, :], condT[:, :, :], leak[:, :, :], ALU.mult).then_inc(leaked_ready, 1)

            def round_(k):
                lstm, scan, done, moe = k, k + -1, k + -2, k + 2
                for u in range(STEPS):
                    if lstm.real():
                        pool.wait_ge(h2_ready, lstm.count(STEPS, u + 1))
                        pool.tensor_tensor(h_lo[:, (u + 1) % 2], h2[:, lstm.ring, :, u, :], h_hi[:, (u + 1) % 2],
                                           ALU.subtract).then_inc(lo_ready, 1)
                    if scan.real():
                        pool.wait_ge(s_hist_ready, scan.count(STEPS, u + 1))
                        pool.tensor_tensor(s_lo[:, (u + 1) % 2], s_hist[:, scan.ring, :, u, :],
                                           s_hi[:, (u + 1) % 2], ALU.subtract).then_inc(s_lo_ready, 1)
                        pool.tensor_tensor(leaked[:, :, :], s_hist[:, scan.ring, :, u, :], leak[:, :, :],
                                           ALU.mult).then_inc(leaked_ready, 1)
                    if u == 1 and moe.real():
                        pool.wait_ge(logits_ready, moe.count(1, 1))
                        pool.tensor_tensor(exp_neg[:, :], euler[:, :], neg_logits[:, :], ALU.pow)\
                            .then_inc(exp_ready, 1)
                    if u == 0 and done.real():
                        wait(pool, y_turned, done.count(1))
                        pool.wait_ge(s_hist_ready, done.count(STEPS, STEPS))
                        for h in range(KD):
                            pool.tensor_tensor(y[:, h].rearrange("p b t -> p t b"), z[:, done.ring, h],
                                               s_hist[:, done.ring, h], ALU.add).then_inc(y_ready, 1)

            rounds(pool, round_)

        @block.scalar
        def _(act):
            def load(dst, src, s):
                act.dma_start(dst, src).then_inc(s, 16)

            for n, v in enumerate((L0_b1, L0_b2, L3_alpha)):
                load(vec_rows[KD * n:KD * (n + 1), :], v.rearrange("(o p) -> o p", p=P), w_gate)
            load(routerW[:, :, :], router_W.rearrange("(k p) e -> p k e", p=P), w_gate)
            load(router_bias[:, :], router_b.partition_broadcast(P), w_gate)
            for row in (0, 32, 64):
                load(bias_row[row:row + 1, 0:4 * D], lstm_b.partition_broadcast(1), w_lstm)
                load(bias_row[row:row + 1, 4 * D:NB], L3_b.partition_broadcast(1), w_lstm)

            for n in range(2):
                act.wait_ge(gate_chain, GC_PRE[n])
                act.activation(sig[:, n], pre[:, n], ACT.Tanh, scale=0.5).then_inc(act_ready, 1)
            act.wait_ge(ps_ready, PR_LEAK)
            for dst, ps in ((Ws, gates_ps[0]), (Wz, gates_ps[1])):
                act.activation(dst[:, :, :].rearrange("p k n -> p (k n)"),
                               ps[:, 0:4, :].rearrange("p a n -> p (a n)"), ACT.Copy, scale=SCALE)\
                   .then_inc(act_ready, 1)

            def moe_slot(c, u, slot):
                for q in range(UNITS):
                    if c.real() and ACT_AT[q] == (u, slot):
                        act.wait_ge(up_done, c.count(UNITS, q + 1))
                        a = up_ps[q % 2][:, 0:2, :].rearrange("p a n -> p (a n)")
                        if q < SHARED:
                            act.activation(gate_tanh[:, q, :], a, ACT.Tanh, scale=0.5).then_inc(tanh_ready, 1)
                        else:
                            act.wait_ge(down_done, c.count(UNITS, q - 1))
                            act.activation(hid[:, q % 2].rearrange("p a n -> p (a n)"), a, ACT.Gelu)\
                               .then_inc(gelu_done, 1)

            def round_(k):
                lstm, scan, moe, done = k, k + -1, k + 2, k + -2
                for u in range(STEPS):
                    if lstm.real():
                        act.wait_ge(gates_done, lstm.count(STEPS, u + 1))
                        act.activation(cell_gates[:, u % 2, 0:4 * HB].rearrange("p (j b) -> p j b", b=B),
                                       gates_ps[lstm.ring][:, :, u * B:(u + 1) * B], ACT.Tanh,
                                       scale=0.5 / SCALE).then_inc(gates_act, 1)
                    moe_slot(moe, u, 0)
                    if lstm.real():
                        act.wait_ge(cell_done, lstm.count(STEPS, u + 1))
                        act.activation(tanh_c[:, :], cell_gates[:, (u + 1) % 2, 4 * HB:5 * HB], ACT.Tanh,
                                       scale=0.5).then_inc(tanh_done, 1)
                    if scan.real():
                        act.wait_ge(s_done, scan.count(STEPS, u + 1))
                        act.activation(s_gate[:, :, :], scan_ps[:, 0:KD, u * B:(u + 1) * B], ACT.Tanh,
                                       scale=0.5 / SCALE).then_inc(s_sig, 1)
                        act.wait_ge(s_pre_done, scan.count(STEPS, u + 1))
                        act.activation(s_hi[:, (u + 1) % 2], s_pre[:, :, :], ACT.Tanh).then_inc(s_hi_ready, 1)
                        act.activation(s_hist[:, scan.ring, :, u, :], s_pre[:, :, :], ACT.Tanh)\
                           .then_inc(s_hist_ready, 1)
                    moe_slot(moe, u, 1)
                    if u == 1 and done.real():
                        act.wait_ge(y_turned, done.count(1, 1))
                        wait(act, y_stored[done.ring], done.pairs(16))
                        act.activation(y_out[:, done.ring, :], up_ps[1][:, 0:2, :].rearrange("p a n -> p (a n)"),
                                       ACT.Copy).then_inc(y_out_ready, 1)

            rounds(act, round_)

        @block.vector
        def _(dve):
            links = [0]

            def link(ins):
                links[0] += 1
                ins.then_inc(chain, 1)
                dve.wait_ge(chain, links[0])

            dve.wait_ge(consts, 7)
            dve.wait_ge(ps_ready, PR_COND)
            link(dve.tensor_copy(condT[:, :, :], tok_ps[:, 0:HB].rearrange("p (k b) -> p k b", b=B)))
            link(dve.tensor_scalar(cond2[:, :, :], condT[:, :, :], 2.0, None, ALU.mult))
            dve.tensor_copy(h_hi[:, 0], cond2[:, :, :]).then_inc(hi_ready, 1)
            dve.tensor_copy(s_hi[:, 0], condT[:, :, :]).then_inc(s_hi_ready, 1)
            link(dve.tensor_copy(vecs[:, :], tok_ps[:, HB:HB + 3 * KD]))
            link(dve.tensor_scalar(keep[:, :], vecs[:, 2 * KD:3 * KD], -1.0, 1.0, ALU.mult, ALU.add))
            link(dve.tensor_copy(leak[:, :, :], keep[:, :].unsqueeze(2).broadcast_to([P, KD, B])))
            assert links[0] == CH_STATE
            dve.wait_ge(ps_ready, PR_TURNED)
            dve.tensor_copy(gateW1T[:, :, :].rearrange("p k n -> p (k n)"),
                            up_ps[0][:, :, :].rearrange("p a n -> p (a n)")).then_inc(gate_chain, 1)
            dve.tensor_copy(gateW2T[:, :, :].rearrange("p k n -> p (k n)"),
                            up_ps[1][:, :, :].rearrange("p a n -> p (a n)")).then_inc(gate_chain, 1)
            for k in range(KD):
                dve.tensor_copy(cond_tok[:, k], condT[:, k].unsqueeze(1).broadcast_to([P, STEPS, B]))\
                   .then_inc(gate_chain, 1)
            for n in range(2):
                dve.wait_ge(ps_ready, PR_GATE[n])
                for o in range(KD):
                    dve.tensor_scalar(pre[:, n, o], tok_ps[:, 32 + HB * n + B * o:32 + HB * n + B * (o + 1)],
                                      (1.0, 0.5)[n], vecs[:, KD * n + o:KD * n + o + 1], ALU.mult, ALU.add)\
                       .then_inc(gate_chain, 1)
                dve.wait_ge(act_ready, n + 1)
                if n == 0:
                    dve.wait_ge(gate_chain, GC_PRE[0])
                    dve.scalar_tensor_tensor(out=hid_gate[:, :, :], in0=sig[:, 0], scalar=1.0, in1=pre[:, 0],
                                             op0=ALU.add, op1=ALU.mult).then_inc(gate_chain, 1)
                    dve.tensor_copy(cond_logits[:, :], tok_ps[:, 128:128 + E]).then_inc(gate_chain, 1)
                else:
                    link(dve.tensor_scalar(two_plus_gate[:, :, :], sig[:, 1], 0.5, 2.5, ALU.mult, ALU.add))

            def scan_weights():
                G = 3 * D
                dve.wait_ge(w_lstm, W_LSTM)
                dve.wait_ge(act_ready, 4)
                link(dve.tensor_scalar(Wx_sb[:, :, 0:G], Wx_sb[:, :, 0:G], SCALE, None, ALU.mult))
                link(dve.tensor_scalar(Wx_sb[:, :, G:4 * D], Wx_sb[:, :, G:4 * D], 2 * SCALE, None, ALU.mult))
                link(dve.tensor_scalar(Wh_sb[:, :, 0:G], Wh_sb[:, :, 0:G], 0.5 * SCALE, None, ALU.mult))
                link(dve.tensor_scalar(Wh_sb[:, :, G:4 * D], Wh_sb[:, :, G:4 * D], SCALE, None, ALU.mult))
                for w, hi, lo in ((Wh_sb, Wh_hi, Wh_lo), (Ws, Ws_hi, Ws_lo)):
                    link(dve.tensor_copy(hi[:, :, :], w[:, :, :]))
                    link(dve.tensor_tensor(lo[:, :, :], w[:, :, :], hi[:, :, :], ALU.subtract))
                for row in (0, 32, 64):
                    r = slice(row, row + 1)
                    link(dve.tensor_scalar(bias_row[r, 0:G], bias_row[r, 0:G], SCALE, None, ALU.mult))
                    link(dve.tensor_scalar(bias_row[r, G:4 * D], bias_row[r, G:4 * D], 2 * SCALE, None, ALU.mult))
                    link(dve.tensor_scalar(bias_row[r, 4 * D:NB], bias_row[r, 4 * D:NB], SCALE, None, ALU.mult))
                    if row == 0:
                        link(dve.tensor_copy(bias_parts[r, :], bias_row[r, :]))
                        continue
                    link(dve.tensor_copy(bias_1[r, :], bias_row[r, :]))
                    link(dve.tensor_tensor(bias_r1[r, :], bias_row[r, :], bias_1[r, :], ALU.subtract))
                    if row == 32:
                        link(dve.tensor_copy(bias_parts[r, :], bias_r1[r, :]))
                        continue
                    link(dve.tensor_copy(bias_2[r, :], bias_r1[r, :]))
                    link(dve.tensor_tensor(bias_r2[r, :], bias_r1[r, :], bias_2[r, :], ALU.subtract))
                    link(dve.tensor_copy(bias_parts[r, :], bias_r2[r, :]))
                dve.engine_nop().then_inc(lstm_w_ready, 1)

            def routed(c, n, ins):
                ins.then_inc(route, 1)
                dve.wait_ge(route, c.count(ROUTE, n + 1))

            def routing(c, u, slot):
                if (u, slot) == (1, 0):
                    dve.wait_ge(router_done, c.count(1, 1))
                    dve.scalar_tensor_tensor(out=neg_logits[:, :], in0=tok_ps[:, 0:E], scalar=-1.0,
                                             in1=cond_logits[:, :], op0=ALU.mult, op1=ALU.subtract)\
                       .then_inc(logits_ready, 1)
                if (u, slot) == (2, 1):
                    dve.wait_ge(exp_ready, c.count(1, 1))
                    routed(c, 0, dve.tensor_scalar(exp_plus[:, :], exp_neg[:, :], 1.0, None, ALU.add))
                    routed(c, 1, dve.reciprocal(scores[:, :], exp_plus[:, :]))
                if (u, slot) == (3, 1):
                    routed(c, 2, dve.tensor_tensor(biased[:, :], scores[:, :], router_bias[:, :], ALU.add))
                    dve.tensor_copy(took_wait[:, :], biased[:, 0:1])
                    routed(c, 3, dve.max(out=best[:, :], in_=biased[:, :]))
                if (u, slot) == (4, 0):
                    dve.tensor_copy(took_wait[:, :], best[:, 0:1])
                    routed(c, 4, dve.max_index(best_at[:, :], best[:, :], biased[:, :]))
                    routed(c, 5, dve.tensor_copy(best_atf[:, :], best_at[:, 0:2]))
                if (u, slot) == (4, 1):
                    dve.tensor_scalar(is_first[:, :], expert_row[:, :], best_atf[:, 0:1], None,
                                      ALU.is_equal).then_inc(route, 1)
                    dve.wait_ge(route, c.count(ROUTE, 7))
                    routed(c, 7, dve.scalar_tensor_tensor(out=chosen[:, :], in0=expert_row[:, :],
                                                          scalar=best_atf[:, 1:2], in1=is_first[:, :],
                                                          op0=ALU.is_equal, op1=ALU.add))
                if (u, slot) == (5, 0):
                    routed(c, 8, dve.scalar_tensor_tensor(out=chosen_scores[:, :], in0=scores[:, :], scalar=1.0,
                                                          in1=chosen[:, :], op0=ALU.mult, op1=ALU.mult,
                                                          accum_out=denom[:, :]))
                if (u, slot) == (5, 1):
                    routed(c, 9, dve.tensor_scalar(denom_eps[:, :], denom[:, :], 1e-9, None, ALU.add))
                    dve.tensor_scalar(even[:, :], denom[:, :], 1e-9, 0.5, ALU.is_le, ALU.mult)
                    routed(c, 10, dve.reciprocal(recip[:, :], denom_eps[:, :]))
                if (u, slot) == (6, 0):
                    routed(c, 11, dve.scalar_tensor_tensor(out=norm[:, :], in0=denom[:, :], scalar=1e-9,
                                                           in1=recip[:, :], op0=ALU.is_gt, op1=ALU.mult))
                    dve.tensor_scalar(evened[:, :], chosen[:, :], even[:, 0:1], None, ALU.mult).then_inc(route, 1)
                if (u, slot) == (6, 1):
                    dve.wait_ge(route, c.count(ROUTE, 13))
                    dve.scalar_tensor_tensor(out=combine[:, c.ring, :], in0=chosen_scores[:, :],
                                             scalar=norm[:, 0:1], in1=evened[:, :], op0=ALU.mult, op1=ALU.add)\
                       .then_inc(route, 1)

            def sum_unit(c, q):
                dve.wait_ge(down_done, c.count(UNITS, q + 1))
                got = tok_ps[:, 0:D]
                if q == 0:
                    ins = dve.tensor_copy(moe_sum[:, :], got)
                elif q < SHARED:
                    dve.wait_ge(sum_done, c.count(UNITS, q))
                    ins = dve.tensor_tensor(moe_sum[:, :], got, moe_sum[:, :], ALU.add)
                else:
                    if q == SHARED:
                        dve.wait_ge(route, c.count(ROUTE, ROUTE))
                    dve.wait_ge(sum_done, c.count(UNITS, q))
                    ins = dve.scalar_tensor_tensor(out=moe_sum[:, :], in0=got,
                                                   scalar=combine[:, c.ring, q - SHARED:q - SHARED + 1],
                                                   in1=moe_sum[:, :], op0=ALU.mult, op1=ALU.add)
                ins.then_inc(sum_done, 1)

            def glu_unit(c, q):
                dve.wait_ge(tanh_ready, c.count(SHARED, q + 1))
                ps = up_ps[q % 2]
                dve.scalar_tensor_tensor(out=glu_tmp[:, :], in0=gate_tanh[:, q, :], scalar=1.0,
                                         in1=ps[:, 0:2, :].rearrange("p a n -> p (a n)"),
                                         op0=ALU.add, op1=ALU.mult).then_inc(glu_half, 1)
                dve.wait_ge(glu_half, c.count(SHARED, q + 1))
                dve.scalar_tensor_tensor(out=hid[:, q % 2].rearrange("p a n -> p (a n)"), in0=glu_tmp[:, :],
                                         scalar=0.5, in1=ps[:, 2:4, :].rearrange("p a n -> p (a n)"),
                                         op0=ALU.mult, op1=ALU.mult).then_inc(glu_done, 1)

            def moe_slot(c, u, slot):
                if not c.real():
                    return
                if (u, slot) == (0, 1):
                    dve.wait_ge(x_turned, c.count(1, 1))
                    for h in range(KD):
                        ins = dve.tensor_tensor(x1T[:, c.ring, h].rearrange("p (t b) -> p t b", b=B),
                                                up_ps[0][:, h, :].rearrange("p (b t) -> p t b", b=B),
                                                two_plus_gate[:, h].unsqueeze(1).broadcast_to([P, STEPS, B]),
                                                ALU.mult)
                    ins.then_inc(x1_ready, 1)
                for q in range(UNITS):
                    if SUM_AT[q] == (u, slot):
                        sum_unit(c, q)
                routing(c, u, slot)
                for q in range(SHARED):
                    if GLU_AT[q] == (u, slot):
                        glu_unit(c, q)

            def round_(k):
                lstm, scan, moe, fin = k, k + -1, k + 2, k + 1
                if k.i is None and k.c == -1:
                    scan_weights()
                for u in range(STEPS):
                    if u == 0 and scan.real():
                        dve.wait_ge(h2_ready, scan.count(STEPS, STEPS))
                        dve.scalar_tensor_tensor(
                            out=z[:, scan.ring].rearrange("p k t b -> p (k t b)"),
                            in0=h2[:, scan.ring].rearrange("p k t b -> p (k t b)"), scalar=0.5,
                            in1=x2T[:, scan.ring].rearrange("p k n -> p (k n)"),
                            op0=ALU.mult, op1=ALU.add).then_inc(z_ready, 1)
                    if lstm.real():
                        now, then = cell_gates[:, u % 2], cell_gates[:, (u + 1) % 2]
                        dve.wait_ge(gates_act, lstm.count(STEPS, u + 1))
                        dve.scalar_tensor_tensor(out=parts[:, :], in0=now[:, 0:2 * HB], scalar=1.0,
                                                 in1=now[:, 3 * HB:5 * HB], op0=ALU.add, op1=ALU.mult)\
                           .then_inc(parts_done, 1)
                        dve.wait_ge(parts_done, lstm.count(STEPS, u + 1))
                        dve.scalar_tensor_tensor(out=then[:, 4 * HB:5 * HB], in0=parts[:, HB:2 * HB], scalar=0.5,
                                                 in1=parts[:, 0:HB], op0=ALU.mult, op1=ALU.add)\
                           .then_inc(cell_done, 1)
                    if u == 0 and fin.real():
                        sum_unit(fin, UNITS - 1)
                    moe_slot(moe, u, 0)
                    if lstm.real():
                        dve.wait_ge(tanh_done, lstm.count(STEPS, u + 1))
                        o = now[:, 2 * HB:3 * HB].rearrange("p (k b) -> p k b", b=B)
                        tc = tanh_c[:, :].rearrange("p (k b) -> p k b", b=B)
                        dve.scalar_tensor_tensor(out=h_hi[:, (u + 1) % 2], in0=o, scalar=1.0, in1=tc,
                                                 op0=ALU.add, op1=ALU.mult).then_inc(hi_ready, 1)
                        dve.scalar_tensor_tensor(out=h2[:, lstm.ring, :, u, :], in0=o, scalar=1.0, in1=tc,
                                                 op0=ALU.add, op1=ALU.mult).then_inc(h2_ready, 1)
                    if scan.real():
                        dve.wait_ge(s_sig, scan.count(STEPS, u + 1))
                        if u == 0:
                            dve.wait_ge(z_ready, scan.count(1, 1))
                        dve.scalar_tensor_tensor(out=gated[:, :, :], in0=s_gate[:, :, :], scalar=1.0,
                                                 in1=z[:, scan.ring, :, u, :], op0=ALU.add, op1=ALU.mult)\
                           .then_inc(s_gated, 1)
                        dve.wait_ge(s_gated, scan.count(STEPS, u + 1))
                        dve.wait_ge(leaked_ready, scan.count(STEPS, u + 1))
                        dve.scalar_tensor_tensor(out=s_pre[:, :, :], in0=gated[:, :, :], scalar=0.5,
                                                 in1=leaked[:, :, :], op0=ALU.mult, op1=ALU.add)\
                           .then_inc(s_pre_done, 1)
                    moe_slot(moe, u, 1)
                    if u == 0 and fin.real():
                        dve.wait_ge(sum_turned, fin.count(1, 1))
                        dve.scalar_tensor_tensor(out=x2T[:, fin.ring].rearrange("p k n -> p (k n)"),
                                                 in0=tok_ps[:, 0:D], scalar=1.0 / 3.0,
                                                 in1=x1T[:, fin.ring].rearrange("p k n -> p (k n)"),
                                                 op0=ALU.mult, op1=ALU.add).then_inc(x2_ready, 1)

            rounds(dve, round_)

        @block.tensor
        def _(pe):
            mm = pe.matmul

            pe.wait_ge(consts, 2)
            pe.wait_ge(w_gate, W_GATE)
            for k in range(KD):
                ins = pe.transpose(tok_ps[:, B * k:B * (k + 1)], cond_sb[:, P * k:P * (k + 1)], ident[0:B, 0:B])
            ins = pe.transpose(tok_ps[:, HB:HB + 3 * KD], vec_rows[:, :], ident[0:3 * KD, 0:3 * KD])
            ins.then_inc(ps_ready, 1)
            for w, ps in ((gateW1, up_ps[0]), (gateW2, up_ps[1])):
                for k in range(KD):
                    for o in range(KD):
                        ins = pe.transpose(ps[:, KD * k + o, :], w[:, o, P * k:P * (k + 1)], ident[:, :])
            ins.then_inc(ps_ready, 1)
            pe.wait_ge(gate_chain, GC_COND)
            for k in range(KD):
                mm(tok_ps[:, 128:128 + E], cond_tok[:, k].rearrange("p t b -> p (t b)"), routerW[:, KD + k, :],
                   start=(k == 0), stop=(k == KD - 1))
            for n, w, src in ((0, gateW1T, condT), (1, gateW2T, hid_gate)):
                if n == 1:
                    pe.wait_ge(gate_chain, GC_HID)
                for o in range(KD):
                    for k in range(KD):
                        at = 32 + HB * n + B * o
                        ins = mm(tok_ps[:, at:at + B], w[:, k, P * o:P * (o + 1)], src[:, k, :],
                                 start=(k == 0), stop=(k == KD - 1))
                ins.then_inc(ps_ready, 1)
            pe.wait_ge(w_lstm, W_LSTM)
            for part, ps in ((0, gates_ps[0]), (1, gates_ps[1])):
                for k in range(KD):
                    for o in range(KD):
                        at = D * part + P * k
                        ins = pe.transpose(ps[:, KD * k + o, :], leakW[:, o, at:at + P], ident[:, :])
            ins.then_inc(ps_ready, 1)

            def add(to, w, a, start=False):
                return mm(to, w, a, start=start, stop=True, skip_group_check=True)

            def gate_inputs(c, u):
                if u == 0:
                    return
                if u == 1:
                    if c.i is None and c.c == 0:
                        pe.wait_ge(lstm_w_ready, 1)
                    pe.wait_ge(x2_ready, c.count(1, 1))
                ps = gates_ps[c.ring]
                j = (u - 1) // 2
                tile = slice(P * j, P * (j + 1))
                if u % 2:
                    add(ps[:, j, :], bias_parts[:, tile], ones[:, :], start=(j % 4 == 0))
                    add(ps[:, j, :], Wx_sb[:, 0, tile], x2T[:, c.ring, 0])
                if u % 2 == 0 or u == STEPS - 1:
                    add(ps[:, j, :], Wx_sb[:, 1, tile], x2T[:, c.ring, 1])

            def scan_inputs(c):
                pe.wait_ge(z_ready, c.count(1, 1))
                wait(pe, s_sig, c.count(STEPS))
                for o in range(KD):
                    add(scan_ps[:, o, :], bias_parts[:, 4 * D + P * o:4 * D + P * (o + 1)], ones[:, :],
                        start=(o == 0))
                    for k in range(KD):
                        add(scan_ps[:, o, :], Wz[:, k, P * o:P * (o + 1)],
                            z[:, c.ring, k].rearrange("p t b -> p (t b)"))

            def recurrent(sums, tiles, W_hi, W_lo, hi, lo, hi_sem, lo_sem, count, done):
                pe.wait_ge(hi_sem, count)
                for j in range(tiles):
                    for k in range(KD):
                        add(sums(j), W_hi[:, k, P * j:P * (j + 1)], hi[:, k, :])
                        add(sums(j), W_lo[:, k, P * j:P * (j + 1)], hi[:, k, :])
                pe.wait_ge(lo_sem, count)
                for j in range(tiles):
                    for k in range(KD):
                        ins = add(sums(j), W_hi[:, k, P * j:P * (j + 1)], lo[:, k, :])
                ins.then_inc(done, 1)

            def piece(c, n):
                if n >= len(PIECES) or PIECES[n] is None:
                    return
                kind, q, part = PIECES[n]
                if kind == "up":
                    ps, rhs = up_ps[q % 2], x1T[:, c.ring]
                    if part == 0:
                        if q < SHARED:
                            if c.i is None and c.c == 0 and q == 0:
                                pe.wait_ge(w_moe, W_MOE)
                            if q == 0:
                                pe.wait_ge(x1_ready, c.count(1, 1))
                            else:
                                wait(pe, y_out_ready, c.count(1, -3))
                        else:
                            wait_hid(pe, c, q - 2)
                    if q < SHARED:
                        w, at = (w1_sb, w3_sb)[part // 2], 2 * P * q + P * (part % 2)
                        lhs = [w[:, k, at:at + P] for k in range(KD)]
                    else:
                        lhs = [W1e_sb[:, q - SHARED, k, P * part:P * (part + 1)] for k in range(KD)]
                    for k in range(KD):
                        ins = mm(ps[:, part, :], lhs[k], rhs[:, k], start=(k == 0), stop=(k == KD - 1))
                    if part == (3 if q < SHARED else 1):
                        ins.then_inc(up_done, 1)
                else:
                    if part == 0:
                        wait_hid(pe, c, q)
                        if q == 0:
                            pe.wait_ge(logits_ready, c.count(1, 1))
                        else:
                            pe.wait_ge(sum_done, c.count(UNITS, q))
                    w = w2_sb[:, 2 * q + part, :] if q < SHARED else W2e_sb[:, q - SHARED, part, :]
                    ins = mm(tok_ps[:, 0:D], hid[:, q % 2, part], w, start=(part == 0), stop=(part == 1))
                    if part == 1:
                        ins.then_inc(down_done, 1)

            def round_(k):
                lstm, scan, moe, fin, done = k, k + -1, k + 2, k + 1, k + -2
                for u in range(STEPS):
                    if lstm.real():
                        ps = gates_ps[lstm.ring]
                        recurrent(lambda j: ps[:, j, u * B:(u + 1) * B], GATES, Wh_hi, Wh_lo, h_hi[:, u % 2],
                                  h_lo[:, u % 2], hi_ready, lo_ready, lstm.count(STEPS, u + 1), gates_done)
                    if u == 0 and moe.real():
                        pe.wait_ge(x_here[moe.ring], moe.pairs(16, 16))
                        wait_hid(pe, moe + -1, UNITS - 2)
                        for h in range(KD):
                            ins = pe.transpose(up_ps[0][:, h, :], x_in[:, moe.ring, P * h:P * (h + 1)], ident[:, :])
                        ins.then_inc(x_turned, 1)
                    if u == 0 and scan.real():
                        scan_inputs(scan)
                    if u == 1 and moe.real():
                        pe.wait_ge(x1_ready, moe.count(1, 1))
                        wait(pe, x2_ready, moe.count(1))
                        for h in range(KD):
                            ins = mm(tok_ps[:, 0:E], x1T[:, moe.ring, h], routerW[:, h, :],
                                     start=(h == 0), stop=(h == KD - 1))
                        ins.then_inc(router_done, 1)
                    if u == 1 and done.real():
                        pe.wait_ge(y_ready, done.count(KD, KD))
                        wait_hid(pe, moe + -1 if moe.real() else Chunk(None, CHUNKS - 1), UNITS - 1)
                        for h in range(KD):
                            ins = pe.transpose(up_ps[1][:, h, :], y[:, h].rearrange("p b t -> p (b t)"), ident[:, :])
                        ins.then_inc(y_turned, 1)
                    if u > 0 and moe.real():
                        piece(moe, 3 * (u - 1))
                    if scan.real():
                        recurrent(lambda j: scan_ps[:, j, u * B:(u + 1) * B], KD, Ws_hi, Ws_lo, s_hi[:, u % 2],
                                  s_lo[:, u % 2], s_hi_ready, s_lo_ready, scan.count(STEPS, u + 1), s_done)
                    if fin.real():
                        if u == 0:
                            pe.wait_ge(sum_done, fin.count(UNITS, UNITS))
                            for h in range(KD):
                                ins = pe.transpose(tok_ps[:, P * h:P * (h + 1)], moe_sum[:, P * h:P * (h + 1)],
                                                   ident[:, :])
                            ins.then_inc(sum_turned, 1)
                        gate_inputs(fin, u)
                    if u > 0 and moe.real():
                        piece(moe, 3 * (u - 1) + 1)
                        piece(moe, 3 * (u - 1) + 2)

            rounds(pe, round_)


PR_COND, PR_TURNED, PR_GATE, PR_LEAK = 1, 2, (3, 4), 5
CH_STATE = 5
GC_COND = 2 + KD
GC_PRE = (GC_COND + KD, GC_COND + KD + 2 + KD)
GC_HID = GC_COND + KD + 2

_NAMES = ["x", "cond_1024", "L0_cond_W1", "L0_cond_b1", "L0_cond_W2", "L0_cond_b2", "L1_cond_router_W",
          "L1_cond_router_bias", "L1_cond_w1", "L1_cond_w3", "L1_cond_w2", "L1_cond_W1e", "L1_cond_W2e",
          "L2_cond_Wx", "L2_cond_Wh", "L2_cond_b", "L3_cond_W", "L3_cond_b", "L3_cond_alpha"]


def kernel(**inputs):
    import concourse.bacc as bacc
    from concourse.bass_utils import run_bass_kernel_spmd

    nc = bacc.Bacc("TRN2", target_bir_lowering=False, num_devices=1)
    arrays, args = {}, []
    for name in _NAMES:
        a = np.ascontiguousarray(inputs[name])
        arrays[name + "_dram"] = a
        args.append(nc.dram_tensor(name + "_dram", a.shape, mybir.dt.from_np(a.dtype), kind="ExternalInput").ap())
    out = nc.dram_tensor("out_dram", (B, T, D), F32, kind="ExternalOutput").ap()
    build(nc, *args, out)
    return run_bass_kernel_spmd(nc, [arrays], core_ids=[0]).results[0]["out_dram"]
```

```python
from contextlib import ExitStack

import numpy as np
import concourse.bass as bass
from concourse import mybir

F32, F16, BF16, U32 = mybir.dt.float32, mybir.dt.float16, mybir.dt.bfloat16, mybir.dt.uint32
ALU = mybir.AluOpType
ACT = mybir.ActivationFunctionType

B, T, D = 8, 512, 256
P = 128
KD = D // P
STEPS = 16
TOK = STEPS * B
CHUNKS = T // STEPS
HS, HE, E = 512, 256, 8
GATES = 4 * KD
SCALE = 256.0

SHARED = 2
UNITS = SHARED + E
PIECES = [("up", q, n) for q in range(SHARED) for n in range(4)]
for q in range(UNITS):
    PIECES += [("down", q, n) for n in range(2)]
    if q + 2 < UNITS:
        PIECES += [("up", q + 2, n) for n in range(2)]
PIECES_AT = [4, 3, 1, 4, 3, 3, 3, 3, 2, 3, 3, 3, 3, 2, 2, 2]
HALVES_AT = [0] * 4 + [1] * 8 + [2] * 4
assert len(PIECES_AT) == len(HALVES_AT) == STEPS
assert sum(PIECES_AT) == len(PIECES) and sum(HALVES_AT) == 2 * GATES
LAG = 2
Z, Z_LOW, SUM_TURN, X2, X2_SPLIT = 0, 1, 1, 2, 3
X_TURN, X1, X1_SPLIT, ROUTER, LOGITS, POW, ROUTING = 2, 3, 4, 4, 5, 6, 7
Y, Y_TURN, Y_STORE = (5, 7), 8, 9


def step_after(kind, q):
    last = max(n for n, p in enumerate(PIECES) if p[:2] == (kind, q))
    return next(u for u in range(STEPS) if last < sum(PIECES_AT[:u + 1])) + 1


GLU_AT = [step_after("up", q) for q in range(SHARED)]
HID_AT = [step_after("up", q) + (q <= SHARED) for q in range(UNITS)]
SUM_AT = [step_after("down", q) for q in range(UNITS)]


class Chunk:

    def __init__(self, i, c):
        self.i, self.c = i, c

    def __add__(self, n):
        return Chunk(self.i, self.c + n)

    @property
    def ring(self):
        return self.c % 2

    def count(self, per_chunk, more=0):
        n = self.c * per_chunk + more
        return n if self.i is None else self.i * (2 * per_chunk) + n

    def pairs(self, per_pair, more=0):
        n = self.c // 2 * per_pair + more
        return n if self.i is None else self.i * per_pair + n

    def real(self):
        return self.i is not None or 0 <= self.c < CHUNKS


def wait(eng, sem, count):
    if not isinstance(count, int) or count > 0:
        eng.wait_ge(sem, count)


def scan_at(k, u):
    return (k + -1, u - LAG) if u >= LAG else (k + -2, u + STEPS - LAG)


def rounds(eng, round_):
    looped = (CHUNKS - 5) // 2
    for k in range(-3, 2):
        round_(Chunk(None, k))
    with eng.Fori(0, looped) as i:
        round_(Chunk(i, 2))
        round_(Chunk(i, 3))
    for k in range(2 + 2 * looped, CHUNKS + 2):
        round_(Chunk(None, k))


def build(nc, x, cond, L0_W1, L0_b1, L0_W2, L0_b2, router_W, router_b, w1, w3, w2, W1e, W2e,
          Wx, Wh, lstm_b, L3_W, L3_b, L3_alpha, out):
    with ExitStack() as ctx:
        def sb(name, shape, dt=F32):
            return ctx.enter_context(nc.sbuf_tensor(name, shape, dt))

        def pb(name, shape):
            return ctx.enter_context(nc.psum_tensor(name, shape, F32))

        def sem(name):
            return ctx.enter_context(nc.semaphore(name))

        ident = sb("ident", [P, P])
        expert_row = sb("expert_row", [P, E])
        euler = sb("euler", [P, E])
        ones = sb("ones", [P, P], BF16)
        gateW1 = sb("gateW1", [P, KD, D])
        gateW2 = sb("gateW2", [P, KD, D])
        gateW1T = sb("gateW1T", [P, KD, D])
        gateW2T = sb("gateW2T", [P, KD, D])
        vec_rows = sb("vec_rows", [3 * KD, P])
        vecs = sb("vecs", [P, 3 * KD])
        routerW = sb("routerW", [P, 2 * KD, E])
        router_bias = sb("router_bias", [P, E])
        w1_sb = sb("w1_sb", [P, KD, HS])
        w3_sb = sb("w3_sb", [P, KD, HS])
        w2_sb = sb("w2_sb", [P, HS // P, D])
        W1e_sb = sb("W1e_sb", [P, E * KD, HE])
        W2e_sb = sb("W2e_sb", [P, E * HE // P, D])
        Wx_sb = sb("Wx_sb", [P, KD, 4 * D])
        Wh_sb = sb("Wh_sb", [P, KD, 4 * D])
        leakW = sb("leakW", [P, KD, 2 * D])

        def pair(name, shape):
            return sb(name + "_hi", shape, F16), sb(name + "_lo", shape, F16)

        w1_p, w3_p, w2_p = pair("w1", [P, KD, HS]), pair("w3", [P, KD, HS]), pair("w2", [P, HS // P, D])
        W1e_p, W2e_p = pair("W1e", [P, E * KD, HE]), pair("W2e", [P, E * HE // P, D])
        Wx_p, Wh_p = pair("Wx", [P, KD, 4 * D]), pair("Wh", [P, KD, 4 * D])
        Ws_p, Wz_p = pair("Ws", [P, KD, D]), pair("Wz", [P, KD, D])
        keep = sb("keep", [P, KD])
        leak = sb("leak", [P, KD, B])
        NB = 4 * D + D
        bias_row = sb("bias_row", [P, NB])
        bias_1 = sb("bias_1", [P, NB], BF16)
        bias_r1 = sb("bias_r1", [P, NB])
        bias_2 = sb("bias_2", [P, NB], BF16)
        bias_r2 = sb("bias_r2", [P, NB])
        bias_parts = sb("bias_parts", [P, NB], BF16)
        cond_sb = sb("cond_sb", [B, D])
        condT = sb("condT", [P, KD, B])
        cond2 = sb("cond2", [P, KD, B])
        cond_tok = sb("cond_tok", [P, KD, STEPS, B])
        pre = sb("pre", [P, 4, KD, B])
        sig = sb("sig", [P, 2, KD, B])
        hid_gate = sb("hid_gate", [P, KD, B])
        two_plus_gate = sb("two_plus_gate", [P, KD, B])
        cond_logits = sb("cond_logits", [P, E])
        x_in = sb("x_in", [P, 2, D])
        x1T = sb("x1T", [P, 2, KD, TOK])
        x2T = sb("x2T", [P, 2, KD, TOK])
        x1_p, x2_p, z_p = pair("x1", [P, 2, KD, TOK]), pair("x2", [P, KD, TOK]), pair("z", [P, KD, TOK])
        gate_tanh = sb("gate_tanh", [P, 2, 2 * TOK])
        glu_tmp = sb("glu_tmp", [P, SHARED, 2 * TOK])
        hid = sb("hid", [P, 2, 2 * TOK])
        hid_p = pair("hid", [P, 2, 2 * TOK])
        moe_sum = sb("moe_sum", [P, D])
        neg_logits = sb("neg_logits", [P, E])
        exp_neg = sb("exp_neg", [P, E])
        exp_plus = sb("exp_plus", [P, E])
        scores = sb("scores", [P, E])
        biased = sb("biased", [P, E])
        best = sb("best", [P, E])
        took_wait = sb("took_wait", [P, 1])
        best_at = sb("best_at", [P, E], U32)
        best_atf = sb("best_atf", [P, 2])
        is_first = sb("is_first", [P, E])
        chosen = sb("chosen", [P, E])
        chosen_scores = sb("chosen_scores", [P, E])
        denom = sb("denom", [P, 1])
        denom_eps = sb("denom_eps", [P, 1])
        recip = sb("recip", [P, 1])
        norm = sb("norm", [P, 1])
        even = sb("even", [P, 1])
        normed = sb("normed", [P, E])
        evened = sb("evened", [P, E])
        combine = sb("combine", [P, 2, E])
        HB = KD * B
        cell_gates = sb("cell_gates", [P, 2, 5 * HB])
        parts = sb("parts", [P, 2 * HB])
        tanh_c = sb("tanh_c", [P, HB])
        h_hi = sb("h_hi", [P, 2, KD, B], F16)
        h_lo = sb("h_lo", [P, 2, KD, B], F16)
        h2 = sb("h2", [P, 2, KD, STEPS, B])
        z = sb("z", [P, 2, KD, STEPS, B])
        s_gate = sb("s_gate", [P, KD, B])
        gated = sb("gated", [P, KD, B])
        leaked = sb("leaked", [P, KD, B])
        s_pre = sb("s_pre", [P, KD, B])
        s_hi = sb("s_hi", [P, 2, KD, B], F16)
        s_lo = sb("s_lo", [P, 2, KD, B], F16)
        s_hist = sb("s_hist", [P, 2, KD, STEPS, B])
        y = sb("y", [P, KD, B, STEPS])
        y_out = sb("y_out", [P, 2, D])

        gates_ps = [pb(f"gates_ps{r}", [P, GATES, TOK]) for r in range(2)]
        up_ps = [pb(f"up_ps{r}", [P, 4, TOK]) for r in range(2)]
        tok_ps = pb("tok_ps", [P, 512])
        scan_ps = pb("scan_ps", [P, 4, TOK])

        w_gate, w_leak, w_bias = sem("w_gate"), sem("w_leak"), sem("w_bias")
        w_here = [sem(f"w_here{n}") for n in range(7)]
        w_high, w_low = sem("w_high"), sem("w_low")
        x_here = [sem("x_here0"), sem("x_here1")]
        y_stored = [sem("y_stored0"), sem("y_stored1")]
        consts = sem("consts")
        chain = sem("chain")
        ps_ready = sem("ps_ready")
        act_ready = sem("act_ready")
        gate_chain = sem("gate_chain")
        bias_zero = sem("bias_zero")
        bias_chain = sem("bias_chain")
        x_turned, x1_ready = sem("x_turned"), sem("x1_ready")
        x1_high, x1_low, x2_high, x2_low = sem("x1_high"), sem("x1_low"), sem("x2_high"), sem("x2_low")
        router_done, logits_ready, exp_ready = sem("router_done"), sem("logits_ready"), sem("exp_ready")
        route = sem("route")
        up_done = sem("up_done")
        tanh_ready, glu_half, glu_done = sem("tanh_ready"), sem("glu_half"), sem("glu_done")
        gelu_done = sem("gelu_done")
        hid_ready = sem("hid_ready")
        down_done, sum_done = sem("down_done"), sem("sum_done")
        sum_turned, x2_ready = sem("sum_turned"), sem("x2_ready")
        gates_done, gates_act = sem("gates_done"), sem("gates_act")
        parts_done, cell_done, tanh_done = sem("parts_done"), sem("cell_done"), sem("tanh_done")
        hi_ready, lo_ready = sem("hi_ready"), sem("lo_ready")
        h2_ready = sem("h2_ready")
        z_ready, z_split = sem("z_ready"), sem("z_split")
        s_done, s_sig, s_gated, s_pre_done = sem("s_done"), sem("s_sig"), sem("s_gated"), sem("s_pre_done")
        s_hi_ready, s_lo_ready, leaked_ready = sem("s_hi_ready"), sem("s_lo_ready"), sem("leaked_ready")
        s_hist_ready = sem("s_hist_ready")
        y_ready, y_turned, y_out_ready = sem("y_ready"), sem("y_turned"), sem("y_out_ready")

        W_GATE = 16 * 8
        ROUTE = 15
        G = 3 * D
        SPLITS = [(w1_p, slice(None), w1_sb, SCALE, 0), (w3_p, slice(None), w3_sb, SCALE, 1),
                  (w2_p, slice(None), w2_sb, SCALE, 2), (W1e_p, slice(None), W1e_sb, SCALE, 3),
                  (W2e_p, slice(None), W2e_sb, SCALE, 4),
                  (Wx_p, slice(0, G), Wx_sb, SCALE, 5), (Wx_p, slice(G, 4 * D), Wx_sb, 2 * SCALE, 5),
                  (Wh_p, slice(0, G), Wh_sb, SCALE / 2, 6), (Wh_p, slice(G, 4 * D), Wh_sb, SCALE, 6)]
        LEAK_SPLITS = [(Ws_p, gates_ps[0]), (Wz_p, gates_ps[1])]
        MOE_SPLITS = 5

        def wait_hid(eng, c, q):
            wait(eng, hid_ready, c.count(UNITS, q + 1))

        block = ctx.enter_context(nc.Block())

        @block.sync
        def _(sp):
            def load(dst, src, s):
                sp.dma_start(dst, src).then_inc(s, 16)

            def load_x(c):
                wait(sp, x_turned, c.count(1, -1))
                src = x[:, bass.ds(c.count(STEPS), STEPS), :]
                sp.dma_start(x_in[:, c.ring, :], src).then_inc(x_here[c.ring], 16)

            load(cond_sb[:, :], cond, w_gate)
            load(gateW1[:, :, :], L0_W1.rearrange("(o p) i -> p o i", p=P), w_gate)
            load(gateW2[:, :, :], L0_W2.rearrange("(o p) i -> p o i", p=P), w_gate)
            load_x(Chunk(None, 0))
            load(w1_sb[:, :, :], w1.rearrange("(k p) n -> p k n", p=P), w_here[0])
            load(w3_sb[:, :, :], w3.rearrange("(k p) n -> p k n", p=P), w_here[1])
            load(w2_sb[:, :, :], w2.rearrange("(k p) n -> p k n", p=P), w_here[2])
            load(W1e_sb[:, :, :], W1e.rearrange("e (k p) n -> p (e k) n", p=P), w_here[3])
            load(W2e_sb[:, :, :], W2e.rearrange("e (k p) n -> p (e k) n", p=P), w_here[4])
            load_x(Chunk(None, 1))
            load(leakW[:, :, :], L3_W.rearrange("(o p) i -> p o i", p=P), w_leak)
            load(Wx_sb[:, :, :], Wx.rearrange("(k p) n -> p k n", p=P), w_here[5])
            load(Wh_sb[:, :, :], Wh.rearrange("(k p) n -> p k n", p=P), w_here[6])

            def round_(k):
                if k.i is not None or k.c >= -1:
                    if (k + 3).real():
                        load_x(k + 3)
                done = k + -2
                if done.real():
                    wait(sp, y_out_ready, done.count(1, 1))
                    dst = out[:, bass.ds(done.count(STEPS), STEPS), :]
                    sp.dma_start(dst, y_out[:, done.ring, :]).then_inc(y_stored[done.ring], 16)

            rounds(sp, round_)
            for r in range(2):
                sp.wait_ge(y_stored[r], 16 * CHUNKS // 2)

        @block.gpsimd
        def _(pool):
            pool.memset(ident[:, :], 0.0).then_inc(consts, 1)
            pool.wait_ge(consts, 1)
            pool.affine_select(out=ident[:, :], in_=ident[:, :], compare_op=ALU.not_equal, fill=1.0,
                               base=0, pattern=[[-1, P]], channel_multiplier=1).then_inc(consts, 1)
            pool.iota(expert_row[:, :], pattern=[[1, E]], base=0, channel_multiplier=0,
                      allow_small_or_imprecise_dtypes=True).then_inc(consts, 1)
            pool.memset(ones[:, :], 1.0).then_inc(consts, 1)
            pool.memset(euler[:, :], float(np.e)).then_inc(consts, 1)
            pool.memset(bias_parts[:, :], 0.0).then_inc(consts, 1)
            pool.memset(cell_gates[:, 0, 4 * HB:5 * HB], 0.0).then_inc(consts, 1)
            pool.memset(bias_row[:, :], 0.0).then_inc(bias_zero, 1)
            pool.wait_ge(chain, CH_STATE)
            pool.wait_ge(hi_ready, 1)
            pool.wait_ge(s_hi_ready, 1)
            pool.tensor_tensor(h_lo[:, 0], cond2[:, :, :], h_hi[:, 0], ALU.subtract).then_inc(lo_ready, 1)
            pool.tensor_tensor(s_lo[:, 0], condT[:, :, :], s_hi[:, 0], ALU.subtract).then_inc(s_lo_ready, 1)
            pool.tensor_tensor(leaked[:, :, :], condT[:, :, :], leak[:, :, :], ALU.mult).then_inc(leaked_ready, 1)

            links = [0]

            def link(ins):
                links[0] += 1
                ins.then_inc(bias_chain, 1)
                pool.wait_ge(bias_chain, links[0])

            pool.wait_ge(w_bias, 16 * 6)
            for cols, factor in ((slice(0, G), SCALE), (slice(G, 4 * D), 2 * SCALE), (slice(4 * D, NB), SCALE)):
                link(pool.tensor_scalar(bias_row[:, cols], bias_row[:, cols], factor, None, ALU.mult))
            link(pool.tensor_copy(bias_1[:, :], bias_row[:, :]))
            link(pool.tensor_tensor(bias_r1[:, :], bias_row[:, :], bias_1[:, :], ALU.subtract))
            link(pool.tensor_copy(bias_2[:, :], bias_r1[:, :]))
            link(pool.tensor_tensor(bias_r2[:, :], bias_r1[:, :], bias_2[:, :], ALU.subtract))
            for row, part in ((0, bias_1), (32, bias_2), (64, bias_r2)):
                link(pool.tensor_copy(bias_parts[row:row + 1, :], part[row:row + 1, :]))
            assert links[0] == BIAS_STEPS

            def round_(k):
                lstm, done, pre, fin = k, k + -2, k + 3, k + 1
                for u in range(STEPS):
                    scan, v = scan_at(k, u)
                    if u == X2_SPLIT and fin.real():
                        pool.wait_ge(x2_high, fin.count(1, 1))
                        pool.tensor_tensor(x2_p[1][:, :, :], x2T[:, fin.ring], x2_p[0][:, :, :], ALU.subtract)\
                            .then_inc(x2_low, 1)
                    if u == X1_SPLIT and pre.real():
                        pool.wait_ge(x1_high, pre.count(1, 1))
                        pool.tensor_tensor(x1_p[1][:, pre.ring], x1T[:, pre.ring], x1_p[0][:, pre.ring],
                                           ALU.subtract).then_inc(x1_low, 1)
                    if u == POW and pre.real():
                        pool.wait_ge(logits_ready, pre.count(1, 1))
                        pool.tensor_tensor(exp_neg[:, :], euler[:, :], neg_logits[:, :], ALU.pow)\
                            .then_inc(exp_ready, 1)
                    if u in Y and done.real():
                        h = Y.index(u)
                        wait(pool, y_turned, done.count(1))
                        pool.wait_ge(s_hist_ready, done.count(STEPS, STEPS))
                        pool.tensor_tensor(y[:, h].rearrange("p b t -> p t b"), z[:, done.ring, h],
                                           s_hist[:, done.ring, h], ALU.add).then_inc(y_ready, 1)
                    if lstm.real():
                        pool.wait_ge(h2_ready, lstm.count(STEPS, u + 1))
                        pool.tensor_tensor(h_lo[:, (u + 1) % 2], h2[:, lstm.ring, :, u, :], h_hi[:, (u + 1) % 2],
                                           ALU.subtract).then_inc(lo_ready, 1)
                    if scan.real():
                        pool.wait_ge(s_hist_ready, scan.count(STEPS, v + 1))
                        pool.tensor_tensor(s_lo[:, (v + 1) % 2], s_hist[:, scan.ring, :, v, :],
                                           s_hi[:, (v + 1) % 2], ALU.subtract).then_inc(s_lo_ready, 1)
                        pool.tensor_tensor(leaked[:, :, :], s_hist[:, scan.ring, :, v, :], leak[:, :, :],
                                           ALU.mult).then_inc(leaked_ready, 1)

            rounds(pool, round_)

        @block.scalar
        def _(act):
            def load(dst, src, s):
                act.dma_start(dst, src).then_inc(s, 16)

            for n, v in enumerate((L0_b1, L0_b2, L3_alpha)):
                load(vec_rows[KD * n:KD * (n + 1), :], v.rearrange("(o p) -> o p", p=P), w_gate)
            load(routerW[:, :, :], router_W.rearrange("(k p) e -> p k e", p=P), w_gate)
            load(router_bias[:, :], router_b.partition_broadcast(P), w_gate)
            act.wait_ge(bias_zero, 1)
            for row in (0, 32, 64):
                load(bias_row[row:row + 1, 0:4 * D], lstm_b.partition_broadcast(1), w_bias)
                load(bias_row[row:row + 1, 4 * D:NB], L3_b.partition_broadcast(1), w_bias)

            for n in range(2):
                act.wait_ge(gate_chain, GC_PRE[n])
                act.activation(sig[:, n], pre[:, n], ACT.Tanh, scale=0.5).then_inc(act_ready, 1)
            def high(dst, src, factor):
                act.activation(dst, src, ACT.Copy, scale=factor).then_inc(w_high, 1)

            def moe_weights():
                for (hi, _), cols, src, factor, n in SPLITS[:MOE_SPLITS]:
                    act.wait_ge(w_here[n], 16)
                    high(hi[:, :, cols], src[:, :, cols], factor)

            def scan_weights():
                for (hi, _), cols, src, factor, n in SPLITS[MOE_SPLITS:]:
                    act.wait_ge(w_here[n], 16)
                    high(hi[:, :, cols], src[:, :, cols], factor)
                act.wait_ge(ps_ready, PR_LEAK)
                for (hi, _), ps in LEAK_SPLITS:
                    high(hi[:, :, :].rearrange("p k n -> p (k n)"),
                         ps[:, 0:4, :].rearrange("p a n -> p (a n)"), SCALE)

            def activate(c, u):
                for q in range(UNITS):
                    if not c.real() or (GLU_AT + HID_AT[SHARED:])[q] != u:
                        continue
                    act.wait_ge(up_done, c.count(UNITS, q + 1))
                    a = up_ps[q % 2][:, 0:2, :].rearrange("p a n -> p (a n)")
                    if q < SHARED:
                        act.activation(gate_tanh[:, q, :], a, ACT.Tanh, scale=0.5 / SCALE)\
                           .then_inc(tanh_ready, 1)
                    else:
                        act.wait_ge(down_done, c.count(UNITS, q - 1))
                        act.activation(hid_p[0][:, q % 2, :], a, ACT.Gelu, scale=1.0 / SCALE)
                        act.activation(hid[:, q % 2, :], a, ACT.Gelu, scale=1.0 / SCALE)\
                           .then_inc(gelu_done, 1)

            def round_(k):
                lstm, moe, done, fin, pre = k, k + 2, k + -2, k + 1, k + 3
                if k.i is None and k.c == -2:
                    moe_weights()
                if k.i is None and k.c == -1:
                    scan_weights()
                for u in range(STEPS):
                    scan, v = scan_at(k, u)
                    activate(moe, u)
                    activate(fin, u + STEPS)
                    if u == Y_STORE and done.real():
                        act.wait_ge(y_turned, done.count(1, 1))
                        wait(act, y_stored[done.ring], done.pairs(16))
                        act.activation(y_out[:, done.ring, :],
                                       gates_ps[fin.ring][:, 6:8, :].rearrange("p a n -> p (a n)"),
                                       ACT.Copy).then_inc(y_out_ready, 1)
                    if u == X2_SPLIT and fin.real():
                        act.wait_ge(x2_ready, fin.count(1, 1))
                        act.activation(x2_p[0][:, :, :], x2T[:, fin.ring], ACT.Copy).then_inc(x2_high, 1)
                    if u == X1_SPLIT and pre.real():
                        act.wait_ge(x1_ready, pre.count(1, 1))
                        act.activation(x1_p[0][:, pre.ring], x1T[:, pre.ring], ACT.Copy).then_inc(x1_high, 1)
                    if lstm.real():
                        act.wait_ge(gates_done, lstm.count(STEPS, u + 1))
                        act.activation(cell_gates[:, u % 2, 0:4 * HB].rearrange("p (j b) -> p j b", b=B),
                                       gates_ps[lstm.ring][:, :, u * B:(u + 1) * B], ACT.Tanh,
                                       scale=0.5 / SCALE).then_inc(gates_act, 1)
                        act.wait_ge(cell_done, lstm.count(STEPS, u + 1))
                        act.activation(tanh_c[:, :], cell_gates[:, (u + 1) % 2, 4 * HB:5 * HB], ACT.Tanh,
                                       scale=0.5).then_inc(tanh_done, 1)
                    if scan.real():
                        act.wait_ge(s_done, scan.count(STEPS, v + 1))
                        act.activation(s_gate[:, :, :], scan_ps[:, 0:KD, v * B:(v + 1) * B], ACT.Tanh,
                                       scale=0.5 / SCALE).then_inc(s_sig, 1)
                        act.wait_ge(s_pre_done, scan.count(STEPS, v + 1))
                        act.activation(s_hi[:, (v + 1) % 2], s_pre[:, :, :], ACT.Tanh).then_inc(s_hi_ready, 1)
                        act.activation(s_hist[:, scan.ring, :, v, :], s_pre[:, :, :], ACT.Tanh)\
                           .then_inc(s_hist_ready, 1)

            rounds(act, round_)

        @block.vector
        def _(dve):
            links = [0]

            def link(ins):
                links[0] += 1
                ins.then_inc(chain, 1)
                dve.wait_ge(chain, links[0])

            dve.wait_ge(consts, 7)
            dve.wait_ge(ps_ready, PR_COND)
            link(dve.tensor_copy(condT[:, :, :], tok_ps[:, 0:HB].rearrange("p (k b) -> p k b", b=B)))
            link(dve.tensor_scalar(cond2[:, :, :], condT[:, :, :], 2.0, None, ALU.mult))
            dve.tensor_copy(h_hi[:, 0], cond2[:, :, :]).then_inc(hi_ready, 1)
            dve.tensor_copy(s_hi[:, 0], condT[:, :, :]).then_inc(s_hi_ready, 1)
            link(dve.tensor_copy(vecs[:, :], tok_ps[:, HB:HB + 3 * KD]))
            link(dve.tensor_scalar(keep[:, :], vecs[:, 2 * KD:3 * KD], -1.0, 1.0, ALU.mult, ALU.add))
            link(dve.tensor_copy(leak[:, :, :], keep[:, :].unsqueeze(2).broadcast_to([P, KD, B])))
            assert links[0] == CH_STATE
            dve.wait_ge(ps_ready, PR_TURNED)
            dve.tensor_copy(gateW1T[:, :, :].rearrange("p k n -> p (k n)"),
                            up_ps[0][:, :, :].rearrange("p a n -> p (a n)")).then_inc(gate_chain, 1)
            dve.tensor_copy(gateW2T[:, :, :].rearrange("p k n -> p (k n)"),
                            up_ps[1][:, :, :].rearrange("p a n -> p (a n)")).then_inc(gate_chain, 1)
            for k in range(KD):
                dve.tensor_copy(cond_tok[:, k], condT[:, k].unsqueeze(1).broadcast_to([P, STEPS, B]))\
                   .then_inc(gate_chain, 1)
            for n in range(2):
                dve.wait_ge(ps_ready, PR_GATE[n])
                for o in range(KD):
                    dve.tensor_scalar(pre[:, n, o], tok_ps[:, 32 + HB * n + B * o:32 + HB * n + B * (o + 1)],
                                      (1.0, 0.5)[n], vecs[:, KD * n + o:KD * n + o + 1], ALU.mult, ALU.add)\
                       .then_inc(gate_chain, 1)
                dve.wait_ge(act_ready, n + 1)
                if n == 0:
                    dve.wait_ge(gate_chain, GC_PRE[0])
                    dve.scalar_tensor_tensor(out=hid_gate[:, :, :], in0=sig[:, 0], scalar=1.0, in1=pre[:, 0],
                                             op0=ALU.add, op1=ALU.mult).then_inc(gate_chain, 1)
                    dve.tensor_copy(cond_logits[:, :], tok_ps[:, 128:128 + E]).then_inc(gate_chain, 1)
                else:
                    link(dve.tensor_scalar(two_plus_gate[:, :, :], sig[:, 1], 0.5, 2.5, ALU.mult, ALU.add))

            highs = [0]

            def low(dst, src, factor, hi):
                highs[0] += 1
                dve.wait_ge(w_high, highs[0])
                dve.scalar_tensor_tensor(out=dst, in0=src, scalar=factor, in1=hi, op0=ALU.mult,
                                         op1=ALU.subtract).then_inc(w_low, 1)

            def moe_weights():
                for (hi, lo), cols, src, factor, n in SPLITS[:MOE_SPLITS]:
                    dve.wait_ge(w_here[n], 16)
                    low(lo[:, :, cols], src[:, :, cols], factor, hi[:, :, cols])

            def scan_weights():
                for (hi, lo), cols, src, factor, n in SPLITS[MOE_SPLITS:]:
                    dve.wait_ge(w_here[n], 16)
                    low(lo[:, :, cols], src[:, :, cols], factor, hi[:, :, cols])
                for (hi, lo), ps in LEAK_SPLITS:
                    low(lo[:, :, :].rearrange("p k n -> p (k n)"), ps[:, 0:4, :].rearrange("p a n -> p (a n)"),
                        SCALE, hi[:, :, :].rearrange("p k n -> p (k n)"))

            def routing(c, u):
                def after(n):
                    dve.wait_ge(route, c.count(ROUTE, n))

                if u == LOGITS:
                    dve.wait_ge(router_done, c.count(1, 1))
                    dve.scalar_tensor_tensor(out=neg_logits[:, :], in0=gates_ps[c.ring][:, 4, 0:E], scalar=-1.0,
                                             in1=cond_logits[:, :], op0=ALU.mult, op1=ALU.subtract)\
                       .then_inc(logits_ready, 1)
                if u == ROUTING:
                    dve.wait_ge(exp_ready, c.count(1, 1))
                    dve.tensor_scalar(exp_plus[:, :], exp_neg[:, :], 1.0, None, ALU.add).then_inc(route, 1)
                    after(1)
                    dve.reciprocal(scores[:, :], exp_plus[:, :]).then_inc(route, 1)
                if u == ROUTING + 1:
                    after(2)
                    dve.tensor_tensor(biased[:, :], scores[:, :], router_bias[:, :], ALU.add).then_inc(route, 1)
                    after(3)
                    dve.tensor_copy(took_wait[:, :], biased[:, 0:1])
                    dve.max(out=best[:, :], in_=biased[:, :]).then_inc(route, 1)
                if u == ROUTING + 2:
                    after(4)
                    dve.tensor_copy(took_wait[:, :], best[:, 0:1])
                    dve.max_index(best_at[:, :], best[:, :], biased[:, :]).then_inc(route, 1)
                    after(5)
                    dve.tensor_copy(best_atf[:, :], best_at[:, 0:2]).then_inc(route, 1)
                if u == ROUTING + 3:
                    after(6)
                    dve.tensor_scalar(is_first[:, :], expert_row[:, :], best_atf[:, 0:1], None,
                                      ALU.is_equal).then_inc(route, 1)
                    after(7)
                    dve.scalar_tensor_tensor(out=chosen[:, :], in0=expert_row[:, :], scalar=best_atf[:, 1:2],
                                             in1=is_first[:, :], op0=ALU.is_equal, op1=ALU.add).then_inc(route, 1)
                if u == ROUTING + 4:
                    after(8)
                    dve.scalar_tensor_tensor(out=chosen_scores[:, :], in0=scores[:, :], scalar=1.0,
                                             in1=chosen[:, :], op0=ALU.mult, op1=ALU.mult,
                                             accum_out=denom[:, :]).then_inc(route, 1)
                if u == ROUTING + 5:
                    after(9)
                    dve.tensor_scalar(denom_eps[:, :], denom[:, :], 1e-9, None, ALU.add).then_inc(route, 1)
                    dve.tensor_scalar(even[:, :], denom[:, :], 1e-9, 0.5, ALU.is_le, ALU.mult).then_inc(route, 1)
                if u == ROUTING + 6:
                    after(11)
                    dve.reciprocal(recip[:, :], denom_eps[:, :]).then_inc(route, 1)
                    dve.tensor_scalar(evened[:, :], chosen[:, :], even[:, 0:1], None, ALU.mult).then_inc(route, 1)
                if u == ROUTING + 7:
                    after(13)
                    dve.scalar_tensor_tensor(out=norm[:, :], in0=denom[:, :], scalar=1e-9, in1=recip[:, :],
                                             op0=ALU.is_gt, op1=ALU.mult).then_inc(route, 1)
                    after(14)
                    dve.scalar_tensor_tensor(out=combine[:, c.ring, :], in0=chosen_scores[:, :],
                                             scalar=norm[:, 0:1], in1=evened[:, :], op0=ALU.mult, op1=ALU.add)\
                       .then_inc(route, 1)

            def sum_unit(c, q):
                dve.wait_ge(down_done, c.count(UNITS, q + 1))
                got = tok_ps[:, 0:D]
                if q == 0:
                    ins = dve.tensor_copy(moe_sum[:, :], got)
                elif q < SHARED:
                    dve.wait_ge(sum_done, c.count(UNITS, q))
                    ins = dve.tensor_tensor(moe_sum[:, :], got, moe_sum[:, :], ALU.add)
                else:
                    if q == SHARED:
                        dve.wait_ge(route, c.count(ROUTE, ROUTE))
                    dve.wait_ge(sum_done, c.count(UNITS, q))
                    ins = dve.scalar_tensor_tensor(out=moe_sum[:, :], in0=got,
                                                   scalar=combine[:, c.ring, q - SHARED:q - SHARED + 1],
                                                   in1=moe_sum[:, :], op0=ALU.mult, op1=ALU.add)
                ins.then_inc(sum_done, 1)

            def hid_unit(c, q):
                hi, lo = hid_p[0][:, q % 2, :], hid_p[1][:, q % 2, :]
                if q < SHARED:
                    dve.wait_ge(glu_half, c.count(SHARED, q + 1))
                    for to in (hi, hid[:, q % 2, :]):
                        ins = dve.scalar_tensor_tensor(out=to, in0=glu_tmp[:, q, :], scalar=0.5 / SCALE ** 2,
                                                       in1=up_ps[q % 2][:, 2:4, :].rearrange("p a n -> p (a n)"),
                                                       op0=ALU.mult, op1=ALU.mult)
                    ins.then_inc(glu_done, 1)
                    dve.wait_ge(glu_done, c.count(SHARED, q + 1))
                else:
                    dve.wait_ge(gelu_done, c.count(E, q - SHARED + 1))
                dve.tensor_tensor(lo, hid[:, q % 2, :], hi, ALU.subtract).then_inc(hid_ready, 1)

            def glu_unit(c, q):
                dve.wait_ge(tanh_ready, c.count(SHARED, q + 1))
                dve.scalar_tensor_tensor(out=glu_tmp[:, q, :], in0=gate_tanh[:, q, :], scalar=1.0,
                                         in1=up_ps[q % 2][:, 0:2, :].rearrange("p a n -> p (a n)"),
                                         op0=ALU.add, op1=ALU.mult).then_inc(glu_half, 1)

            def moe_step(c, u):
                if c.real():
                    for q in range(UNITS):
                        if SUM_AT[q] == u:
                            sum_unit(c, q)
                    for q in range(UNITS):
                        if HID_AT[q] == u:
                            hid_unit(c, q)
                    for q in range(SHARED):
                        if GLU_AT[q] == u:
                            glu_unit(c, q)

            def enter(c, u):
                if u == X1:
                    dve.wait_ge(x_turned, c.count(1, 1))
                    wait(dve, x2_ready, c.count(1, -1))
                    for h in range(KD):
                        ins = dve.tensor_tensor(x1T[:, c.ring, h].rearrange("p (t b) -> p t b", b=B),
                                                gates_ps[c.ring][:, 4 + h, :].rearrange("p (b t) -> p t b", b=B),
                                                two_plus_gate[:, h].unsqueeze(1).broadcast_to([P, STEPS, B]),
                                                ALU.mult)
                    ins.then_inc(x1_ready, 1)
                routing(c, u)

            def round_(k):
                lstm, last, moe, fin, pre = k, k + -1, k + 2, k + 1, k + 3
                if k.i is None and k.c == -2:
                    moe_weights()
                if k.i is None and k.c == -1:
                    scan_weights()
                for u in range(STEPS):
                    scan, v = scan_at(k, u)
                    moe_step(fin, u + STEPS)
                    if u == Z and last.real():
                        dve.wait_ge(h2_ready, last.count(STEPS, STEPS))
                        for to in (z_p[0][:, :, :], z[:, last.ring].rearrange("p k t b -> p k (t b)")):
                            ins = dve.scalar_tensor_tensor(
                                out=to.rearrange("p k n -> p (k n)"),
                                in0=h2[:, last.ring].rearrange("p k t b -> p (k t b)"), scalar=0.5,
                                in1=x2T[:, last.ring].rearrange("p k n -> p (k n)"), op0=ALU.mult, op1=ALU.add)
                        ins.then_inc(z_ready, 1)
                    if u == Z_LOW and last.real():
                        dve.wait_ge(z_ready, last.count(1, 1))
                        dve.tensor_tensor(z_p[1][:, :, :], z[:, last.ring].rearrange("p k t b -> p k (t b)"),
                                          z_p[0][:, :, :], ALU.subtract).then_inc(z_split, 1)
                    if u == X2 and fin.real():
                        dve.wait_ge(sum_turned, fin.count(1, 1))
                        dve.scalar_tensor_tensor(out=x2T[:, fin.ring].rearrange("p k n -> p (k n)"),
                                                 in0=gates_ps[fin.ring][:, 0:2, :].rearrange("p a n -> p (a n)"),
                                                 scalar=1.0 / (3.0 * SCALE),
                                                 in1=x1T[:, fin.ring].rearrange("p k n -> p (k n)"),
                                                 op0=ALU.mult, op1=ALU.add).then_inc(x2_ready, 1)
                    moe_step(moe, u)
                    if lstm.real():
                        now, then = cell_gates[:, u % 2], cell_gates[:, (u + 1) % 2]
                        dve.wait_ge(gates_act, lstm.count(STEPS, u + 1))
                        dve.scalar_tensor_tensor(out=parts[:, :], in0=now[:, 0:2 * HB], scalar=1.0,
                                                 in1=now[:, 3 * HB:5 * HB], op0=ALU.add, op1=ALU.mult)\
                           .then_inc(parts_done, 1)
                        dve.wait_ge(parts_done, lstm.count(STEPS, u + 1))
                        dve.scalar_tensor_tensor(out=then[:, 4 * HB:5 * HB], in0=parts[:, HB:2 * HB], scalar=0.5,
                                                 in1=parts[:, 0:HB], op0=ALU.mult, op1=ALU.add)\
                           .then_inc(cell_done, 1)
                    if pre.real():
                        enter(pre, u)
                    if lstm.real():
                        dve.wait_ge(tanh_done, lstm.count(STEPS, u + 1))
                        o = now[:, 2 * HB:3 * HB].rearrange("p (k b) -> p k b", b=B)
                        tc = tanh_c[:, :].rearrange("p (k b) -> p k b", b=B)
                        dve.scalar_tensor_tensor(out=h_hi[:, (u + 1) % 2], in0=o, scalar=1.0, in1=tc,
                                                 op0=ALU.add, op1=ALU.mult).then_inc(hi_ready, 1)
                        dve.scalar_tensor_tensor(out=h2[:, lstm.ring, :, u, :], in0=o, scalar=1.0, in1=tc,
                                                 op0=ALU.add, op1=ALU.mult).then_inc(h2_ready, 1)
                    if scan.real():
                        dve.wait_ge(s_sig, scan.count(STEPS, v + 1))
                        dve.scalar_tensor_tensor(out=gated[:, :, :], in0=s_gate[:, :, :], scalar=1.0,
                                                 in1=z[:, scan.ring, :, v, :], op0=ALU.add, op1=ALU.mult)\
                           .then_inc(s_gated, 1)
                        dve.wait_ge(s_gated, scan.count(STEPS, v + 1))
                        dve.wait_ge(leaked_ready, scan.count(STEPS, v + 1))
                        dve.scalar_tensor_tensor(out=s_pre[:, :, :], in0=gated[:, :, :], scalar=0.5,
                                                 in1=leaked[:, :, :], op0=ALU.mult, op1=ALU.add)\
                           .then_inc(s_pre_done, 1)

            rounds(dve, round_)

        @block.tensor
        def _(pe):
            mm = pe.matmul

            pe.wait_ge(consts, 2)
            pe.wait_ge(w_gate, W_GATE)
            for k in range(KD):
                ins = pe.transpose(tok_ps[:, B * k:B * (k + 1)], cond_sb[:, P * k:P * (k + 1)], ident[0:B, 0:B])
            ins = pe.transpose(tok_ps[:, HB:HB + 3 * KD], vec_rows[:, :], ident[0:3 * KD, 0:3 * KD])
            ins.then_inc(ps_ready, 1)
            for w, ps in ((gateW1, up_ps[0]), (gateW2, up_ps[1])):
                for k in range(KD):
                    for o in range(KD):
                        ins = pe.transpose(ps[:, KD * k + o, :], w[:, o, P * k:P * (k + 1)], ident[:, :])
            ins.then_inc(ps_ready, 1)
            pe.wait_ge(gate_chain, GC_COND)
            for k in range(KD):
                mm(tok_ps[:, 128:128 + E], cond_tok[:, k].rearrange("p t b -> p (t b)"), routerW[:, KD + k, :],
                   start=(k == 0), stop=(k == KD - 1))
            for n, w, src in ((0, gateW1T, condT), (1, gateW2T, hid_gate)):
                if n == 1:
                    pe.wait_ge(gate_chain, GC_HID)
                for o in range(KD):
                    for k in range(KD):
                        at = 32 + HB * n + B * o
                        ins = mm(tok_ps[:, at:at + B], w[:, k, P * o:P * (o + 1)], src[:, k, :],
                                 start=(k == 0), stop=(k == KD - 1))
                ins.then_inc(ps_ready, 1)
            pe.wait_ge(w_leak, 16)
            for part, ps in ((0, gates_ps[0]), (1, gates_ps[1])):
                for k in range(KD):
                    for o in range(KD):
                        at = D * part + P * k
                        ins = pe.transpose(ps[:, KD * k + o, :], leakW[:, o, at:at + P], ident[:, :])
            ins.then_inc(ps_ready, 1)

            def add(to, w, a, start=False):
                return mm(to, w, a, start=start, stop=True, skip_group_check=True)

            def add_split(to, W, a, start=False):
                add(to, W[0], a[0], start=start)
                add(to, W[1], a[0])
                return add(to, W[0], a[1])

            def gate_inputs(c, u):
                turned, stored = c + 2, c + -3
                if u == HALVES_AT.index(1):
                    if c.i is None and c.c == 0:
                        pe.wait_ge(bias_chain, BIAS_STEPS)
                        pe.wait_ge(w_low, len(SPLITS) + len(LEAK_SPLITS))
                    pe.wait_ge(x2_low, c.count(1, 1))
                ps = gates_ps[c.ring]
                for half in range(sum(HALVES_AT[:u]), sum(HALVES_AT[:u + 1])):
                    j, k = half // 2, half % 2
                    tile = slice(P * j, P * (j + 1))
                    if half == GATES and turned.real():
                        pe.wait_ge(logits_ready, turned.count(1, 1))
                    if half == GATES and stored.real():
                        pe.wait_ge(y_out_ready, stored.count(1, 1))
                    if k == 0:
                        add(ps[:, j, :], bias_parts[:, tile], ones[:, :], start=(j % 4 == 0))
                    add_split(ps[:, j, :], [w[:, k, tile] for w in Wx_p], [x[:, k] for x in x2_p])

            def scan_inputs(c):
                pe.wait_ge(z_split, c.count(1, 1))
                wait(pe, s_sig, c.count(STEPS))
                for o in range(KD):
                    tile = slice(P * o, P * (o + 1))
                    add(scan_ps[:, o, :], bias_parts[:, 4 * D + P * o:4 * D + P * (o + 1)], ones[:, :],
                        start=(o == 0))
                    for k in range(KD):
                        add_split(scan_ps[:, o, :], [w[:, k, tile] for w in Wz_p], [x[:, k] for x in z_p])

            def recurrent(sums, tiles, W, hi, lo, hi_sem, lo_sem, count, done):
                W_hi, W_lo = W
                pe.wait_ge(hi_sem, count)
                for j in range(tiles):
                    for k in range(KD):
                        add(sums(j), W_hi[:, k, P * j:P * (j + 1)], hi[:, k, :])
                        add(sums(j), W_lo[:, k, P * j:P * (j + 1)], hi[:, k, :])
                pe.wait_ge(lo_sem, count)
                for j in range(tiles):
                    for k in range(KD):
                        ins = add(sums(j), W_hi[:, k, P * j:P * (j + 1)], lo[:, k, :])
                ins.then_inc(done, 1)

            def up(c, q, part):
                ps = up_ps[q % 2]
                if part == 0:
                    if q == 0:
                        pe.wait_ge(x1_low, c.count(1, 1))
                    wait_hid(pe, c, q - 2)
                    if c.i is None and c.c == 0:
                        pe.wait_ge(w_low, 2 if q < SHARED else 4)
                for k in range(KD):
                    if q < SHARED:
                        at = 2 * P * q + P * (part % 2)
                        W = [w[:, k, at:at + P] for w in (w1_p, w3_p)[part // 2]]
                    else:
                        W = [w[:, KD * (q - SHARED) + k, P * part:P * (part + 1)] for w in W1e_p]
                    ins = add_split(ps[:, part, :], W, [x[:, c.ring, k] for x in x1_p], start=(part == 0 and k == 0))
                if part == (3 if q < SHARED else 1):
                    ins.then_inc(up_done, 1)

            def down(c, q, part):
                if part == 0:
                    wait_hid(pe, c, q)
                    wait(pe, sum_done, c.count(UNITS, q))
                    if c.i is None and c.c == 0:
                        pe.wait_ge(w_low, 3 if q < SHARED else 5)
                W = [w[:, 2 * q + part, :] for w in w2_p] if q < SHARED else \
                    [w[:, 2 * (q - SHARED) + part, :] for w in W2e_p]
                ins = add_split(tok_ps[:, 0:D], [h[:, q % 2, TOK * part:TOK * (part + 1)] for h in hid_p], W,
                                start=(part == 0))
                if part == 1:
                    ins.then_inc(down_done, 1)

            def piece(c, u, n):
                if c.real() and n < PIECES_AT[u]:
                    kind, q, part = PIECES[sum(PIECES_AT[:u]) + n]
                    (up if kind == "up" else down)(c, q, part)

            def round_(k):
                lstm, last, moe, fin, done, pre = k, k + -1, k + 2, k + 1, k + -2, k + 3
                spare = gates_ps[fin.ring]
                for u in range(STEPS):
                    scan, v = scan_at(k, u)
                    if lstm.real():
                        ps = gates_ps[lstm.ring]
                        recurrent(lambda j: ps[:, j, u * B:(u + 1) * B], GATES, Wh_p, h_hi[:, u % 2],
                                  h_lo[:, u % 2], hi_ready, lo_ready, lstm.count(STEPS, u + 1), gates_done)
                    if u == LAG and last.real():
                        scan_inputs(last)
                    if scan.real():
                        recurrent(lambda j: scan_ps[:, j, v * B:(v + 1) * B], KD, Ws_p, s_hi[:, v % 2],
                                  s_lo[:, v % 2], s_hi_ready, s_lo_ready, scan.count(STEPS, v + 1), s_done)
                    if u == SUM_TURN and fin.real():
                        pe.wait_ge(sum_done, fin.count(UNITS, UNITS))
                        for h in range(KD):
                            ins = pe.transpose(spare[:, h, :], moe_sum[:, P * h:P * (h + 1)], ident[:, :])
                        ins.then_inc(sum_turned, 1)
                    if u == X_TURN and pre.real():
                        pe.wait_ge(x_here[pre.ring], pre.pairs(16, 16))
                        for h in range(KD):
                            ins = pe.transpose(spare[:, 4 + h, :], x_in[:, pre.ring, P * h:P * (h + 1)], ident[:, :])
                        ins.then_inc(x_turned, 1)
                    if u == ROUTER and pre.real():
                        pe.wait_ge(x1_ready, pre.count(1, 1))
                        for h in range(KD):
                            ins = mm(spare[:, 4, 0:E], x1T[:, pre.ring, h], routerW[:, h, :],
                                     start=(h == 0), stop=(h == KD - 1))
                        ins.then_inc(router_done, 1)
                    if u == Y_TURN and done.real():
                        pe.wait_ge(y_ready, done.count(KD, KD))
                        if pre.real():
                            pe.wait_ge(logits_ready, pre.count(1, 1))
                        for h in range(KD):
                            ins = pe.transpose(spare[:, 6 + h, :], y[:, h].rearrange("p b t -> p (b t)"), ident[:, :])
                        ins.then_inc(y_turned, 1)
                    if fin.real():
                        gate_inputs(fin, u)
                    for n in range(PIECES_AT[u]):
                        piece(moe, u, n)

            rounds(pe, round_)


PR_COND, PR_TURNED, PR_GATE, PR_LEAK = 1, 2, (3, 4), 5
CH_STATE = 5
GC_COND = 2 + KD
GC_PRE = (GC_COND + KD, GC_COND + KD + 2 + KD)
BIAS_STEPS = 10
GC_HID = GC_COND + KD + 2

_NAMES = ["x", "cond_1024", "L0_cond_W1", "L0_cond_b1", "L0_cond_W2", "L0_cond_b2", "L1_cond_router_W",
          "L1_cond_router_bias", "L1_cond_w1", "L1_cond_w3", "L1_cond_w2", "L1_cond_W1e", "L1_cond_W2e",
          "L2_cond_Wx", "L2_cond_Wh", "L2_cond_b", "L3_cond_W", "L3_cond_b", "L3_cond_alpha"]


def kernel(**inputs):
    import concourse.bacc as bacc
    from concourse.bass_utils import run_bass_kernel_spmd

    nc = bacc.Bacc("TRN2", target_bir_lowering=False, num_devices=1)
    arrays, args = {}, []
    for name in _NAMES:
        a = np.ascontiguousarray(inputs[name])
        arrays[name + "_dram"] = a
        args.append(nc.dram_tensor(name + "_dram", a.shape, mybir.dt.from_np(a.dtype), kind="ExternalInput").ap())
    out = nc.dram_tensor("out_dram", (B, T, D), F32, kind="ExternalOutput").ap()
    build(nc, *args, out)
    return run_bass_kernel_spmd(nc, [arrays], core_ids=[0]).results[0]["out_dram"]
```

```python
from contextlib import ExitStack

import numpy as np
import concourse.bass as bass
from concourse import mybir

F32, F16, BF16, U32 = mybir.dt.float32, mybir.dt.float16, mybir.dt.bfloat16, mybir.dt.uint32
ALU = mybir.AluOpType
ACT = mybir.ActivationFunctionType

B, T, D = 8, 512, 256
P = 128
KD = D // P
STEPS = 16
TOK = STEPS * B
CHUNKS = T // STEPS
HS, HE, E = 512, 256, 8
GATES = 4 * KD
SCALE = 256.0

SHARED = 2
UNITS = SHARED + E
PIECES = [("up", q, n) for q in range(SHARED) for n in range(4)]
for q in range(UNITS):
    PIECES += [("down", q, n) for n in range(2)]
    if q + 2 < UNITS:
        PIECES += [("up", q + 2, n) for n in range(2)]
PIECES_AT = [4, 3, 2, 3, 3, 3, 3, 3, 2, 3, 2, 3, 3, 3, 2, 2]
HALVES_AT = [0, 0, 0, 0, 1, 1, 1, 1, 1, 1, 1, 1, 2, 1, 2, 3]
assert len(PIECES_AT) == len(HALVES_AT) == STEPS
assert sum(PIECES_AT) == len(PIECES) and sum(HALVES_AT) == 2 * GATES
PART = STEPS // 2
PTOK = PART * B
LAG = PART + 2
Z, Z_LOW, SUM_TURN, X2, X2_SPLIT = 0, 1, 1, 2, 3
X_TURN, X1, X1_SPLIT, ROUTER, LOGITS, POW, ROUTING = 3, 4, 5, 6, 6, 7, 8
Y, Y_TURN, Y_STORE = (5, 6), 8, 9


def step_after(kind, q, first=False):
    pieces = [n for n, p in enumerate(PIECES) if p[:2] == (kind, q)]
    last = pieces[0 if first else -1]
    return next(u for u in range(STEPS) if last < sum(PIECES_AT[:u + 1])) + 1


GLU_AT = [step_after("up", q) for q in range(SHARED)]
HID_AT = [step_after("up", q) + (q <= SHARED) for q in range(UNITS)]
SUM_AT = [step_after("down", q) for q in range(UNITS)]


class Chunk:

    def __init__(self, i, c):
        self.i, self.c = i, c

    def __add__(self, n):
        return Chunk(self.i, self.c + n)

    @property
    def ring(self):
        return self.c % 2

    def count(self, per_chunk, more=0):
        n = self.c * per_chunk + more
        return n if self.i is None else self.i * (2 * per_chunk) + n

    def pairs(self, per_pair, more=0):
        n = self.c // 2 * per_pair + more
        return n if self.i is None else self.i * per_pair + n

    def real(self):
        return self.i is not None or 0 <= self.c < CHUNKS


def wait(eng, sem, count):
    if not isinstance(count, int) or count > 0:
        eng.wait_ge(sem, count)


def scan_at(k, u):
    return (k, u - LAG) if u >= LAG else (k + -1, u + STEPS - LAG)


def part_at(k, u, step):
    return {step: (k + -1, 1), step + PART: (k, 0)}.get(u, (Chunk(None, -1), 0))


def rounds(eng, round_):
    looped = (CHUNKS - 5) // 2
    for k in range(-3, 2):
        round_(Chunk(None, k))
    with eng.Fori(0, looped) as i:
        round_(Chunk(i, 2))
        round_(Chunk(i, 3))
    for k in range(2 + 2 * looped, CHUNKS + 2):
        round_(Chunk(None, k))


def build(nc, x, cond, L0_W1, L0_b1, L0_W2, L0_b2, router_W, router_b, w1, w3, w2, W1e, W2e,
          Wx, Wh, lstm_b, L3_W, L3_b, L3_alpha, out):
    with ExitStack() as ctx:
        def sb(name, shape, dt=F32):
            return ctx.enter_context(nc.sbuf_tensor(name, shape, dt))

        def pb(name, shape):
            return ctx.enter_context(nc.psum_tensor(name, shape, F32))

        def sem(name):
            return ctx.enter_context(nc.semaphore(name))

        ident = sb("ident", [P, P])
        expert_row = sb("expert_row", [P, E])
        euler = sb("euler", [P, E])
        pick = sb("pick", [P, 5 * KD], BF16)
        pick_tok = sb("pick_tok", [P, 5 * KD, TOK], BF16)
        gateW1 = sb("gateW1", [P, KD, D])
        gateW2 = sb("gateW2", [P, KD, D])
        gateW1T = sb("gateW1T", [P, KD, D])
        gateW2T = sb("gateW2T", [P, KD, D])
        vec_rows = sb("vec_rows", [3 * KD, P])
        vecs = sb("vecs", [P, 3 * KD])
        routerW = sb("routerW", [P, 2 * KD, E])
        router_bias = sb("router_bias", [P, E])
        w1_sb = sb("w1_sb", [P, KD, HS])
        w3_sb = sb("w3_sb", [P, KD, HS])
        w2_sb = sb("w2_sb", [P, HS // P, D])
        W1e_sb = sb("W1e_sb", [P, E * KD, HE])
        W2e_sb = sb("W2e_sb", [P, E * HE // P, D])
        Wx_sb = sb("Wx_sb", [P, KD, 4 * D])
        Wh_sb = sb("Wh_sb", [P, KD, 4 * D])
        leakW = sb("leakW", [P, KD, 2 * D])

        def pair(name, shape):
            return sb(name + "_hi", shape, F16), sb(name + "_lo", shape, F16)

        w1_p, w3_p, w2_p = pair("w1", [P, KD, HS]), pair("w3", [P, KD, HS]), pair("w2", [P, HS // P, D])
        W1e_p, W2e_p = pair("W1e", [P, E * KD, HE]), pair("W2e", [P, E * HE // P, D])
        Wx_p, Wh_p = pair("Wx", [P, KD, 4 * D]), pair("Wh", [P, KD, 4 * D])
        router_p = pair("router", [P, KD, E])
        Ws_p, Wz_p = pair("Ws", [P, KD, D]), pair("Wz", [P, KD, D])
        keep = sb("keep", [P, KD])
        leak = sb("leak", [P, KD, B])
        NB = 5 * KD
        bias_row = sb("bias_row", [P, P])
        bias_factor = sb("bias_factor", [P, 1])
        bias_1 = sb("bias_1", [P, P], BF16)
        bias_r1 = sb("bias_r1", [P, P])
        bias_2 = sb("bias_2", [P, P], BF16)
        bias_r2 = sb("bias_r2", [P, P])
        bias_parts = sb("bias_parts", [P, P], BF16)
        cond_sb = sb("cond_sb", [B, D])
        condT = sb("condT", [P, KD, B])
        cond2 = sb("cond2", [P, KD, B])
        cond_tok = sb("cond_tok", [P, KD, STEPS, B])
        pre = sb("pre", [P, 4, KD, B])
        sig = sb("sig", [P, 2, KD, B])
        hid_gate = sb("hid_gate", [P, KD, B])
        two_plus_gate = sb("two_plus_gate", [P, KD, B])
        cond_logits = sb("cond_logits", [P, E])
        x_in = sb("x_in", [P, 2, D])
        x1T = sb("x1T", [P, 2, KD, TOK])
        x2T = sb("x2T", [P, 2, KD, TOK])
        x1_p, x2_p, z_p = pair("x1", [P, 2, KD, TOK]), pair("x2", [P, KD, TOK]), pair("z", [P, KD, TOK])
        gate_tanh = sb("gate_tanh", [P, 2, 2 * TOK])
        glu_tmp = sb("glu_tmp", [P, SHARED, 2 * TOK])
        hid = sb("hid", [P, 2, 2 * TOK])
        hid_p = pair("hid", [P, 2, 2 * TOK])
        moe_sum = sb("moe_sum", [P, D])
        neg_logits = sb("neg_logits", [P, E])
        exp_neg = sb("exp_neg", [P, E])
        exp_plus = sb("exp_plus", [P, E])
        scores = sb("scores", [P, E])
        biased = sb("biased", [P, E])
        best = sb("best", [P, E])
        took_wait = sb("took_wait", [P, 1])
        table_in = sb("table_in", [P, 1])
        best_at = sb("best_at", [P, E], U32)
        best_atf = sb("best_atf", [P, 2])
        is_first = sb("is_first", [P, E])
        chosen = sb("chosen", [P, E])
        chosen_scores = sb("chosen_scores", [P, E])
        denom = sb("denom", [P, 1])
        denom_eps = sb("denom_eps", [P, 1])
        recip = sb("recip", [P, 1])
        norm = sb("norm", [P, 1])
        even = sb("even", [P, 1])
        evened = sb("evened", [P, E])
        combine = sb("combine", [P, 2, E])
        HB = KD * B
        cell_gates = sb("cell_gates", [P, 2, 5 * HB])
        parts = sb("parts", [P, 2 * HB])
        tanh_c = sb("tanh_c", [P, HB])
        h_hi = sb("h_hi", [P, 2, KD, B], F16)
        h_lo = sb("h_lo", [P, 2, KD, B], F16)
        h2 = sb("h2", [P, 2, KD, STEPS, B])
        z = sb("z", [P, 2, KD, STEPS, B])
        s_gate = sb("s_gate", [P, KD, B])
        gated = sb("gated", [P, KD, B])
        leaked = sb("leaked", [P, KD, B])
        s_pre = sb("s_pre", [P, KD, B])
        s_hi = sb("s_hi", [P, 2, KD, B], F16)
        s_lo = sb("s_lo", [P, 2, KD, B], F16)
        s_hist = sb("s_hist", [P, 2, KD, STEPS, B])
        y = sb("y", [P, KD, B, STEPS])
        y_out = sb("y_out", [P, 2, D])

        gates_ps = [pb(f"gates_ps{r}", [P, GATES, TOK]) for r in range(2)]
        up_ps = [pb(f"up_ps{r}", [P, 4, TOK]) for r in range(2)]
        tok_ps = pb("tok_ps", [P, 512])
        scan_ps = pb("scan_ps", [P, 4, TOK])

        w_gate, w_leak, w_bias = sem("w_gate"), sem("w_leak"), sem("w_bias")
        w_here = [sem(f"w_here{n}") for n in range(7)]
        w_high, w_low = sem("w_high"), sem("w_low")
        x_here = [sem("x_here0"), sem("x_here1")]
        y_stored = [sem("y_stored0"), sem("y_stored1")]
        consts = sem("consts")
        chain = sem("chain")
        ps_ready = sem("ps_ready")
        act_ready = sem("act_ready")
        gate_chain = sem("gate_chain")
        bias_zero = sem("bias_zero")
        pick_ready, pick_tok_ready = sem("pick_ready"), sem("pick_tok_ready")
        bias_chain = sem("bias_chain")
        x_turned, x1_ready = sem("x_turned"), sem("x1_ready")
        x1_high, x1_low, x2_high, x2_low = sem("x1_high"), sem("x1_low"), sem("x2_high"), sem("x2_low")
        router_done, logits_ready, exp_ready = sem("router_done"), sem("logits_ready"), sem("exp_ready")
        route = sem("route")
        up_done = sem("up_done")
        tanh_ready, glu_half, glu_done = sem("tanh_ready"), sem("glu_half"), sem("glu_done")
        gelu_done, hid_ready = sem("gelu_done"), sem("hid_ready")
        down_done, sum_done = sem("down_done"), sem("sum_done")
        sum_turned, x2_ready = sem("sum_turned"), sem("x2_ready")
        gates_done, gates_act = sem("gates_done"), sem("gates_act")
        parts_done, cell_done, tanh_done = sem("parts_done"), sem("cell_done"), sem("tanh_done")
        hi_ready, lo_ready = sem("hi_ready"), sem("lo_ready")
        h2_ready = sem("h2_ready")
        z_ready, z_split = sem("z_ready"), sem("z_split")
        s_done, s_sig, s_gated, s_pre_done = sem("s_done"), sem("s_sig"), sem("s_gated"), sem("s_pre_done")
        s_hi_ready, s_lo_ready, leaked_ready = sem("s_hi_ready"), sem("s_lo_ready"), sem("leaked_ready")
        s_hist_ready = sem("s_hist_ready")
        y_ready, y_turned, y_out_ready = sem("y_ready"), sem("y_turned"), sem("y_out_ready")

        W_GATE = 16 * 8
        ROUTE = 15
        G = 3 * D
        leak_ps = gates_ps[1]
        turned_leak = leak_ps[:, :, :].rearrange("p (k o) n -> p k (o n)", o=KD)
        every = slice(None)

        def first_step(kind, q):
            return step_after(kind, q, first=True) - 1

        SPLITS = [("w1", w1_p, every, every, w1_sb, SCALE, (w_here[0], 16), None),
                  ("w3", w3_p, every, every, w3_sb, SCALE, (w_here[1], 16), None),
                  ("w2", w2_p, every, every, w2_sb, SCALE, (w_here[2], 16), None),
                  ("router", router_p, every, every, routerW[:, 0:KD], SCALE, (w_gate, W_GATE), None)]
        for e in range(E):
            tiles = slice(KD * e, KD * (e + 1))
            SPLITS += [(f"W1e_{e}", W1e_p, tiles, every, W1e_sb, SCALE, (w_here[3], 16),
                        (-3, POW) if e < 2 else (-2, first_step("up", SHARED + e) - 2)),
                       (f"W2e_{e}", W2e_p, tiles, every, W2e_sb, SCALE, (w_here[4], 16),
                        (-3, POW) if e < 1 else (-2, first_step("down", SHARED + e) - 2))]
        for gate in range(4):
            cols, double = slice(D * gate, D * (gate + 1)), 2 if D * gate == G else 1
            SPLITS += [(f"Wx_{gate}", Wx_p, every, cols, Wx_sb, double * SCALE, (w_here[5], 16), (-1, gate)),
                       (f"Wh_{gate}", Wh_p, every, cols, Wh_sb, double * SCALE / 2, (w_here[6], 16), (-1, 6 + gate))]
        SPLITS += [("Ws", Ws_p, every, every, turned_leak[:, 0:KD], SCALE, (ps_ready, PR_LEAK), (-1, 10)),
                   ("Wz", Wz_p, every, every, turned_leak[:, KD:2 * KD], SCALE, (ps_ready, PR_LEAK), (-1, 11))]
        SPLITS.sort(key=lambda split: split[-1] or (-4, 0))

        def split_count(name):
            return [split[0] for split in SPLITS].index(name) + 1

        def splits_at(k, u):
            at = (k.c, u) if k and k.i is None else None
            for n, (_, (hi, lo), mid, cols, src, factor, arrival, when) in enumerate(SPLITS):
                if when == at and (at or not k):
                    yield n + 1, src[:, mid, cols], hi[:, mid, cols], lo[:, mid, cols], factor, arrival

        def wait_hid(eng, c, q):
            wait(eng, hid_ready, c.count(UNITS, q + 1))

        block = ctx.enter_context(nc.Block())

        @block.sync
        def _(sp):
            def load(dst, src, s):
                sp.dma_start(dst, src).then_inc(s, 16)

            def load_x(c):
                wait(sp, x_turned, c.count(1, -1))
                src = x[:, bass.ds(c.count(STEPS), STEPS), :]
                sp.dma_start(x_in[:, c.ring, :], src).then_inc(x_here[c.ring], 16)

            load(cond_sb[:, :], cond, w_gate)
            load(gateW1[:, :, :], L0_W1.rearrange("(o p) i -> p o i", p=P), w_gate)
            load(gateW2[:, :, :], L0_W2.rearrange("(o p) i -> p o i", p=P), w_gate)
            load_x(Chunk(None, 0))
            load(w1_sb[:, :, :], w1.rearrange("(k p) n -> p k n", p=P), w_here[0])
            load(w3_sb[:, :, :], w3.rearrange("(k p) n -> p k n", p=P), w_here[1])
            load(w2_sb[:, :, :], w2.rearrange("(k p) n -> p k n", p=P), w_here[2])
            load(W1e_sb[:, :, :], W1e.rearrange("e (k p) n -> p (e k) n", p=P), w_here[3])
            load(W2e_sb[:, :, :], W2e.rearrange("e (k p) n -> p (e k) n", p=P), w_here[4])
            load_x(Chunk(None, 1))
            load(leakW[:, :, :], L3_W.rearrange("(o p) i -> p o i", p=P), w_leak)
            load(Wx_sb[:, :, :], Wx.rearrange("(k p) n -> p k n", p=P), w_here[5])
            load(Wh_sb[:, :, :], Wh.rearrange("(k p) n -> p k n", p=P), w_here[6])

            def round_(k):
                if k.i is not None or k.c >= -1:
                    if (k + 3).real():
                        load_x(k + 3)
                done = k + -2
                if done.real():
                    wait(sp, y_out_ready, done.count(1, 1))
                    dst = out[:, bass.ds(done.count(STEPS), STEPS), :]
                    sp.dma_start(dst, y_out[:, done.ring, :]).then_inc(y_stored[done.ring], 16)

            rounds(sp, round_)
            for r in range(2):
                sp.wait_ge(y_stored[r], 16 * CHUNKS // 2)

        @block.gpsimd
        def _(pool):
            pool.memset(ident[:, :], 0.0).then_inc(consts, 1)
            pool.wait_ge(consts, 1)
            pool.affine_select(out=ident[:, :], in_=ident[:, :], compare_op=ALU.not_equal, fill=1.0,
                               base=0, pattern=[[-1, P]], channel_multiplier=1).then_inc(consts, 1)
            pool.iota(expert_row[:, :], pattern=[[1, E]], base=0, channel_multiplier=0,
                      allow_small_or_imprecise_dtypes=True).then_inc(consts, 1)
            pool.memset(bias_row[:, :], 0.0).then_inc(bias_zero, 1)
            pool.memset(euler[:, :], float(np.e)).then_inc(consts, 1)
            pool.memset(bias_parts[:, :], 0.0).then_inc(consts, 1)
            pool.memset(cell_gates[:, 0, 4 * HB:5 * HB], 0.0).then_inc(consts, 1)
            pool.wait_ge(chain, CH_STATE)
            pool.wait_ge(hi_ready, 1)
            pool.wait_ge(s_hi_ready, 1)
            pool.tensor_tensor(h_lo[:, 0], cond2[:, :, :], h_hi[:, 0], ALU.subtract).then_inc(lo_ready, 1)
            pool.tensor_tensor(s_lo[:, 0], condT[:, :, :], s_hi[:, 0], ALU.subtract).then_inc(s_lo_ready, 1)
            pool.tensor_tensor(leaked[:, :, :], condT[:, :, :], leak[:, :, :], ALU.mult).then_inc(leaked_ready, 1)

            def split_biases():
                links = [0]

                def link(ins):
                    links[0] += 1
                    ins.then_inc(bias_chain, 1)
                    pool.wait_ge(bias_chain, links[0])

                pool.wait_ge(pick_ready, 1)
                pool.wait_ge(w_bias, 16 * 6)
                link(pool.tensor_tensor(bias_factor[:, :], pick[:, 3 * KD:3 * KD + 1], pick[:, 3 * KD + 1:4 * KD],
                                        ALU.add))
                link(pool.tensor_scalar(bias_factor[:, :], bias_factor[:, :], SCALE, SCALE, ALU.mult, ALU.add))
                link(pool.tensor_scalar(bias_row[:, :], bias_row[:, :], bias_factor[:, 0:1], None, ALU.mult))
                link(pool.tensor_copy(bias_1[:, :], bias_row[:, :]))
                link(pool.tensor_tensor(bias_r1[:, :], bias_row[:, :], bias_1[:, :], ALU.subtract))
                link(pool.tensor_copy(bias_2[:, :], bias_r1[:, :]))
                link(pool.tensor_tensor(bias_r2[:, :], bias_r1[:, :], bias_2[:, :], ALU.subtract))
                for row, part in ((0, bias_1), (32, bias_2), (64, bias_r2)):
                    link(pool.tensor_copy(bias_parts[row:row + 32, :], part[row:row + 32, :]))
                assert links[0] == BIAS_STEPS

            def round_(k):
                lstm, done, pre, fin = k, k + -2, k + 3, k + 1
                for u in range(STEPS):
                    scan, v = scan_at(k, u)
                    if u == X2_SPLIT and fin.real():
                        pool.wait_ge(x2_high, fin.count(1, 1))
                        pool.tensor_tensor(x2_p[1][:, :, :], x2T[:, fin.ring], x2_p[0][:, :, :], ALU.subtract)\
                            .then_inc(x2_low, 1)
                    if u == X1_SPLIT and pre.real():
                        pool.wait_ge(x1_high, pre.count(1, 1))
                        pool.tensor_tensor(x1_p[1][:, pre.ring], x1T[:, pre.ring], x1_p[0][:, pre.ring],
                                           ALU.subtract).then_inc(x1_low, 1)
                    if u == POW and pre.real():
                        pool.wait_ge(logits_ready, pre.count(1, 1))
                        pool.tensor_tensor(exp_neg[:, :], euler[:, :], neg_logits[:, :], ALU.pow)\
                            .then_inc(exp_ready, 1)
                    if u in Y and done.real():
                        h = Y.index(u)
                        wait(pool, y_turned, done.count(1))
                        pool.wait_ge(s_hist_ready, done.count(STEPS, STEPS))
                        pool.tensor_tensor(y[:, h].rearrange("p b t -> p t b"), z[:, done.ring, h],
                                           s_hist[:, done.ring, h], ALU.add).then_inc(y_ready, 1)
                    if lstm.real():
                        pool.wait_ge(h2_ready, lstm.count(STEPS, u + 1))
                        pool.tensor_tensor(h_lo[:, (u + 1) % 2], h2[:, lstm.ring, :, u, :], h_hi[:, (u + 1) % 2],
                                           ALU.subtract).then_inc(lo_ready, 1)
                    if scan.real():
                        pool.wait_ge(s_hist_ready, scan.count(STEPS, v + 1))
                        pool.tensor_tensor(s_lo[:, (v + 1) % 2], s_hist[:, scan.ring, :, v, :],
                                           s_hi[:, (v + 1) % 2], ALU.subtract).then_inc(s_lo_ready, 1)
                        pool.tensor_tensor(leaked[:, :, :], s_hist[:, scan.ring, :, v, :], leak[:, :, :],
                                           ALU.mult).then_inc(leaked_ready, 1)
                if k.i is None and k.c == -2:
                    split_biases()

            rounds(pool, round_)

        @block.scalar
        def _(act):
            def load(dst, src, s):
                act.dma_start(dst, src).then_inc(s, 16)

            for n, v in enumerate((L0_b1, L0_b2, L3_alpha)):
                load(vec_rows[KD * n:KD * (n + 1), :], v.rearrange("(o p) -> o p", p=P), w_gate)
            load(routerW[:, :, :], router_W.rearrange("(k p) e -> p k e", p=P), w_gate)
            load(router_bias[:, :], router_b.partition_broadcast(P), w_gate)
            act.wait_ge(bias_zero, 1)
            for row in (0, 32, 64):
                load(bias_row[row:row + GATES, :], lstm_b.rearrange("(j p) -> j p", p=P), w_bias)
                load(bias_row[row + GATES:row + NB, :], L3_b.rearrange("(j p) -> j p", p=P), w_bias)

            def split_high(k, u=None):
                for _, src, hi, _, factor, arrival in splits_at(k, u):
                    act.wait_ge(*arrival)
                    act.activation(hi, src, ACT.Copy, scale=factor).then_inc(w_high, 1)

            act.wait_ge(consts, CONSTS)
            act.activation(table_in[:, :], cell_gates[:, 0, 4 * HB:4 * HB + 1], ACT.Gelu)
            split_high(None)
            for n in range(2):
                act.wait_ge(gate_chain, GC_PRE[n])
                act.activation(sig[:, n], pre[:, n], ACT.Tanh, scale=0.5).then_inc(act_ready, 1)
            def activate(c, u):
                for q in range(UNITS):
                    if not c.real() or (GLU_AT + HID_AT[SHARED:])[q] != u:
                        continue
                    act.wait_ge(up_done, c.count(UNITS, q + 1))
                    a = up_ps[q % 2][:, 0:2, :].rearrange("p a n -> p (a n)")
                    if q < SHARED:
                        act.activation(gate_tanh[:, q, :], a, ACT.Tanh, scale=0.5 / SCALE)\
                           .then_inc(tanh_ready, 1)
                    else:
                        act.wait_ge(down_done, c.count(UNITS, q - 1))
                        act.activation(hid_p[0][:, q % 2, :], a, ACT.Gelu, scale=1.0 / SCALE)
                        act.activation(hid[:, q % 2, :], a, ACT.Gelu, scale=1.0 / SCALE)\
                           .then_inc(gelu_done, 1)

            def round_(k):
                lstm, moe, done, fin, pre = k, k + 2, k + -2, k + 1, k + 3
                for u in range(STEPS):
                    scan, v = scan_at(k, u)
                    split_high(k, u)
                    activate(moe, u)
                    activate(fin, u + STEPS)
                    if u == Y_STORE and done.real():
                        act.wait_ge(y_turned, done.count(1, 1))
                        wait(act, y_stored[done.ring], done.pairs(16))
                        act.activation(y_out[:, done.ring, :],
                                       gates_ps[fin.ring][:, 6:8, :].rearrange("p a n -> p (a n)"),
                                       ACT.Copy).then_inc(y_out_ready, 1)
                    if u == X2_SPLIT and fin.real():
                        act.wait_ge(x2_ready, fin.count(1, 1))
                        act.activation(x2_p[0][:, :, :], x2T[:, fin.ring], ACT.Copy).then_inc(x2_high, 1)
                    if u == X1_SPLIT and pre.real():
                        act.wait_ge(x1_ready, pre.count(1, 1))
                        act.activation(x1_p[0][:, pre.ring], x1T[:, pre.ring], ACT.Copy).then_inc(x1_high, 1)
                    if lstm.real():
                        act.wait_ge(gates_done, lstm.count(STEPS, u + 1))
                        act.activation(cell_gates[:, u % 2, 0:4 * HB].rearrange("p (j b) -> p j b", b=B),
                                       gates_ps[lstm.ring][:, :, u * B:(u + 1) * B], ACT.Tanh,
                                       scale=0.5 / SCALE).then_inc(gates_act, 1)
                        act.wait_ge(cell_done, lstm.count(STEPS, u + 1))
                        act.activation(tanh_c[:, :], cell_gates[:, (u + 1) % 2, 4 * HB:5 * HB], ACT.Tanh,
                                       scale=0.5).then_inc(tanh_done, 1)
                    if scan.real():
                        act.wait_ge(s_done, scan.count(STEPS, v + 1))
                        act.activation(s_gate[:, :, :], scan_ps[:, 0:KD, v * B:(v + 1) * B], ACT.Tanh,
                                       scale=0.5 / SCALE).then_inc(s_sig, 1)
                        act.wait_ge(s_pre_done, scan.count(STEPS, v + 1))
                        act.activation(s_hi[:, (v + 1) % 2], s_pre[:, :, :], ACT.Tanh).then_inc(s_hi_ready, 1)
                        act.activation(s_hist[:, scan.ring, :, v, :], s_pre[:, :, :], ACT.Tanh)\
                           .then_inc(s_hist_ready, 1)

            rounds(act, round_)

        @block.vector
        def _(dve):
            links = [0]

            def link(ins):
                links[0] += 1
                ins.then_inc(chain, 1)
                dve.wait_ge(chain, links[0])

            def split_low(k, u=None):
                for count, src, hi, lo, factor, arrival in splits_at(k, u):
                    dve.wait_ge(*arrival)
                    dve.wait_ge(w_high, count)
                    dve.scalar_tensor_tensor(out=lo, in0=src, scalar=factor, in1=hi, op0=ALU.mult,
                                             op1=ALU.subtract).then_inc(w_low, 1)

            dve.wait_ge(consts, CONSTS)
            link(dve.tensor_tensor(pick[:, :], ident[:, 0:NB], ident[:, 32:32 + NB], ALU.add))
            dve.tensor_tensor(pick[:, :], pick[:, :], ident[:, 64:64 + NB], ALU.add).then_inc(pick_ready, 1)
            dve.wait_ge(pick_ready, 1)
            dve.tensor_copy(pick_tok[:, :, :], pick[:, :].unsqueeze(2).broadcast_to([P, NB, TOK]))\
               .then_inc(pick_tok_ready, 1)
            dve.wait_ge(ps_ready, PR_COND)
            link(dve.tensor_copy(condT[:, :, :], tok_ps[:, 0:HB].rearrange("p (k b) -> p k b", b=B)))
            link(dve.tensor_scalar(cond2[:, :, :], condT[:, :, :], 2.0, None, ALU.mult))
            dve.tensor_copy(h_hi[:, 0], cond2[:, :, :]).then_inc(hi_ready, 1)
            dve.tensor_copy(s_hi[:, 0], condT[:, :, :]).then_inc(s_hi_ready, 1)
            link(dve.tensor_copy(vecs[:, :], tok_ps[:, HB:HB + 3 * KD]))
            link(dve.tensor_scalar(keep[:, :], vecs[:, 2 * KD:3 * KD], -1.0, 1.0, ALU.mult, ALU.add))
            link(dve.tensor_copy(leak[:, :, :], keep[:, :].unsqueeze(2).broadcast_to([P, KD, B])))
            assert links[0] == CH_STATE
            dve.wait_ge(ps_ready, PR_TURNED)
            dve.tensor_copy(gateW1T[:, :, :].rearrange("p k n -> p (k n)"),
                            up_ps[0][:, :, :].rearrange("p a n -> p (a n)")).then_inc(gate_chain, 1)
            dve.tensor_copy(gateW2T[:, :, :].rearrange("p k n -> p (k n)"),
                            up_ps[1][:, :, :].rearrange("p a n -> p (a n)")).then_inc(gate_chain, 1)
            for k in range(KD):
                dve.tensor_copy(cond_tok[:, k], condT[:, k].unsqueeze(1).broadcast_to([P, STEPS, B]))\
                   .then_inc(gate_chain, 1)
            split_low(None)
            for n in range(2):
                dve.wait_ge(ps_ready, PR_GATE[n])
                for o in range(KD):
                    dve.tensor_scalar(pre[:, n, o], tok_ps[:, 32 + HB * n + B * o:32 + HB * n + B * (o + 1)],
                                      (1.0, 0.5)[n], vecs[:, KD * n + o:KD * n + o + 1], ALU.mult, ALU.add)\
                       .then_inc(gate_chain, 1)
                dve.wait_ge(act_ready, n + 1)
                if n == 0:
                    dve.wait_ge(gate_chain, GC_PRE[0])
                    dve.scalar_tensor_tensor(out=hid_gate[:, :, :], in0=sig[:, 0], scalar=1.0, in1=pre[:, 0],
                                             op0=ALU.add, op1=ALU.mult).then_inc(gate_chain, 1)
                    dve.tensor_copy(cond_logits[:, :], tok_ps[:, 128:128 + E]).then_inc(gate_chain, 1)
                else:
                    link(dve.tensor_scalar(two_plus_gate[:, :, :], sig[:, 1], 0.5, 2.5, ALU.mult, ALU.add))

            def routing(c, u):
                def after(n):
                    dve.wait_ge(route, c.count(ROUTE, n))

                if u == LOGITS:
                    dve.wait_ge(router_done, c.count(1, 1))
                    dve.scalar_tensor_tensor(out=neg_logits[:, :], in0=gates_ps[c.ring][:, 4, 0:E],
                                             scalar=-1.0 / SCALE,
                                             in1=cond_logits[:, :], op0=ALU.mult, op1=ALU.subtract)\
                       .then_inc(logits_ready, 1)
                if u == ROUTING:
                    dve.wait_ge(exp_ready, c.count(1, 1))
                    dve.tensor_scalar(exp_plus[:, :], exp_neg[:, :], 1.0, None, ALU.add).then_inc(route, 1)
                    after(1)
                    dve.reciprocal(scores[:, :], exp_plus[:, :]).then_inc(route, 1)
                if u == ROUTING + 1:
                    after(2)
                    dve.tensor_tensor(biased[:, :], scores[:, :], router_bias[:, :], ALU.add).then_inc(route, 1)
                    after(3)
                    dve.tensor_copy(took_wait[:, :], biased[:, 0:1])
                    dve.max(out=best[:, :], in_=biased[:, :]).then_inc(route, 1)
                if u == ROUTING + 2:
                    after(4)
                    dve.tensor_copy(took_wait[:, :], best[:, 0:1])
                    dve.max_index(best_at[:, :], best[:, :], biased[:, :]).then_inc(route, 1)
                    after(5)
                    dve.tensor_copy(best_atf[:, :], best_at[:, 0:2]).then_inc(route, 1)
                if u == ROUTING + 3:
                    after(6)
                    dve.tensor_scalar(is_first[:, :], expert_row[:, :], best_atf[:, 0:1], None,
                                      ALU.is_equal).then_inc(route, 1)
                    after(7)
                    dve.scalar_tensor_tensor(out=chosen[:, :], in0=expert_row[:, :], scalar=best_atf[:, 1:2],
                                             in1=is_first[:, :], op0=ALU.is_equal, op1=ALU.add).then_inc(route, 1)
                if u == ROUTING + 4:
                    after(8)
                    dve.scalar_tensor_tensor(out=chosen_scores[:, :], in0=scores[:, :], scalar=1.0,
                                             in1=chosen[:, :], op0=ALU.mult, op1=ALU.mult,
                                             accum_out=denom[:, :]).then_inc(route, 1)
                if u == ROUTING + 5:
                    after(9)
                    dve.tensor_scalar(denom_eps[:, :], denom[:, :], 1e-9, None, ALU.add).then_inc(route, 1)
                    dve.tensor_scalar(even[:, :], denom[:, :], 1e-9, 0.5, ALU.is_le, ALU.mult).then_inc(route, 1)
                if u == ROUTING + 6:
                    after(11)
                    dve.reciprocal(recip[:, :], denom_eps[:, :]).then_inc(route, 1)
                    dve.tensor_scalar(evened[:, :], chosen[:, :], even[:, 0:1], None, ALU.mult).then_inc(route, 1)
                if u == ROUTING + 7:
                    after(13)
                    dve.scalar_tensor_tensor(out=norm[:, :], in0=denom[:, :], scalar=1e-9, in1=recip[:, :],
                                             op0=ALU.is_gt, op1=ALU.mult).then_inc(route, 1)
                    after(14)
                    dve.scalar_tensor_tensor(out=combine[:, c.ring, :], in0=chosen_scores[:, :],
                                             scalar=norm[:, 0:1], in1=evened[:, :], op0=ALU.mult, op1=ALU.add)\
                       .then_inc(route, 1)

            def sum_unit(c, q):
                dve.wait_ge(down_done, c.count(UNITS, q + 1))
                got = tok_ps[:, 0:D]
                if q == 0:
                    ins = dve.tensor_copy(moe_sum[:, :], got)
                elif q < SHARED:
                    dve.wait_ge(sum_done, c.count(UNITS, q))
                    ins = dve.tensor_tensor(moe_sum[:, :], got, moe_sum[:, :], ALU.add)
                else:
                    if q == SHARED:
                        dve.wait_ge(route, c.count(ROUTE, ROUTE))
                    dve.wait_ge(sum_done, c.count(UNITS, q))
                    ins = dve.scalar_tensor_tensor(out=moe_sum[:, :], in0=got,
                                                   scalar=combine[:, c.ring, q - SHARED:q - SHARED + 1],
                                                   in1=moe_sum[:, :], op0=ALU.mult, op1=ALU.add)
                ins.then_inc(sum_done, 1)

            def hid_unit(c, q):
                hi, lo = hid_p[0][:, q % 2, :], hid_p[1][:, q % 2, :]
                if q < SHARED:
                    dve.wait_ge(glu_half, c.count(SHARED, q + 1))
                    for to in (hi, hid[:, q % 2, :]):
                        ins = dve.scalar_tensor_tensor(out=to, in0=glu_tmp[:, q, :], scalar=0.5 / SCALE ** 2,
                                                       in1=up_ps[q % 2][:, 2:4, :].rearrange("p a n -> p (a n)"),
                                                       op0=ALU.mult, op1=ALU.mult)
                    ins.then_inc(glu_done, 1)
                    dve.wait_ge(glu_done, c.count(SHARED, q + 1))
                else:
                    dve.wait_ge(gelu_done, c.count(E, q - SHARED + 1))
                dve.tensor_tensor(lo, hid[:, q % 2, :], hi, ALU.subtract).then_inc(hid_ready, 1)

            def glu_unit(c, q):
                dve.wait_ge(tanh_ready, c.count(SHARED, q + 1))
                dve.scalar_tensor_tensor(out=glu_tmp[:, q, :], in0=gate_tanh[:, q, :], scalar=1.0,
                                         in1=up_ps[q % 2][:, 0:2, :].rearrange("p a n -> p (a n)"),
                                         op0=ALU.add, op1=ALU.mult).then_inc(glu_half, 1)

            def moe_step(c, u):
                if c.real():
                    for q in range(UNITS):
                        if SUM_AT[q] == u:
                            sum_unit(c, q)
                    for q in range(UNITS):
                        if HID_AT[q] == u:
                            hid_unit(c, q)
                    for q in range(SHARED):
                        if GLU_AT[q] == u:
                            glu_unit(c, q)

            def enter(c, u):
                if u == X1:
                    dve.wait_ge(x_turned, c.count(1, 1))
                    wait(dve, x2_ready, c.count(1, -1))
                    for h in range(KD):
                        ins = dve.tensor_tensor(x1T[:, c.ring, h].rearrange("p (t b) -> p t b", b=B),
                                                gates_ps[c.ring][:, 4 + h, :].rearrange("p (b t) -> p t b", b=B),
                                                two_plus_gate[:, h].unsqueeze(1).broadcast_to([P, STEPS, B]),
                                                ALU.mult)
                    ins.then_inc(x1_ready, 1)
                routing(c, u)

            def round_(k):
                lstm, moe, fin, pre = k, k + 2, k + 1, k + 3
                for u in range(STEPS):
                    scan, v = scan_at(k, u)
                    split_low(k, u)
                    moe_step(fin, u + STEPS)
                    part, half = part_at(k, u, Z)
                    if part.real():
                        steps, toks = slice(PART * half, PART * (half + 1)), slice(PTOK * half, PTOK * (half + 1))
                        dve.wait_ge(h2_ready, part.count(STEPS, PART * (half + 1)))
                        if half == 0:
                            wait(dve, y_ready, part.count(KD, -KD))
                        for to in (z_p[0][:, :, toks], z[:, part.ring, :, steps, :].rearrange("p k t b -> p k (t b)")):
                            ins = dve.scalar_tensor_tensor(
                                out=to, in0=h2[:, part.ring, :, steps, :].rearrange("p k t b -> p k (t b)"),
                                scalar=0.5, in1=x2T[:, part.ring, :, toks], op0=ALU.mult, op1=ALU.add)
                        ins.then_inc(z_ready, 1)
                    part, half = part_at(k, u, Z_LOW)
                    if part.real():
                        steps, toks = slice(PART * half, PART * (half + 1)), slice(PTOK * half, PTOK * (half + 1))
                        dve.wait_ge(z_ready, part.count(2, half + 1))
                        dve.tensor_tensor(z_p[1][:, :, toks],
                                          z[:, part.ring, :, steps, :].rearrange("p k t b -> p k (t b)"),
                                          z_p[0][:, :, toks], ALU.subtract).then_inc(z_split, 1)
                    if u == X2 and fin.real():
                        dve.wait_ge(sum_turned, fin.count(1, 1))
                        dve.scalar_tensor_tensor(out=x2T[:, fin.ring].rearrange("p k n -> p (k n)"),
                                                 in0=gates_ps[fin.ring][:, 0:2, :].rearrange("p a n -> p (a n)"),
                                                 scalar=1.0 / (3.0 * SCALE),
                                                 in1=x1T[:, fin.ring].rearrange("p k n -> p (k n)"),
                                                 op0=ALU.mult, op1=ALU.add).then_inc(x2_ready, 1)
                    moe_step(moe, u)
                    if lstm.real():
                        now, then = cell_gates[:, u % 2], cell_gates[:, (u + 1) % 2]
                        dve.wait_ge(gates_act, lstm.count(STEPS, u + 1))
                        dve.scalar_tensor_tensor(out=parts[:, :], in0=now[:, 0:2 * HB], scalar=1.0,
                                                 in1=now[:, 3 * HB:5 * HB], op0=ALU.add, op1=ALU.mult)\
                           .then_inc(parts_done, 1)
                        dve.wait_ge(parts_done, lstm.count(STEPS, u + 1))
                        dve.scalar_tensor_tensor(out=then[:, 4 * HB:5 * HB], in0=parts[:, HB:2 * HB], scalar=0.5,
                                                 in1=parts[:, 0:HB], op0=ALU.mult, op1=ALU.add)\
                           .then_inc(cell_done, 1)
                    if pre.real():
                        enter(pre, u)
                    if lstm.real():
                        dve.wait_ge(tanh_done, lstm.count(STEPS, u + 1))
                        o = now[:, 2 * HB:3 * HB].rearrange("p (k b) -> p k b", b=B)
                        tc = tanh_c[:, :].rearrange("p (k b) -> p k b", b=B)
                        dve.scalar_tensor_tensor(out=h_hi[:, (u + 1) % 2], in0=o, scalar=1.0, in1=tc,
                                                 op0=ALU.add, op1=ALU.mult).then_inc(hi_ready, 1)
                        dve.scalar_tensor_tensor(out=h2[:, lstm.ring, :, u, :], in0=o, scalar=1.0, in1=tc,
                                                 op0=ALU.add, op1=ALU.mult).then_inc(h2_ready, 1)
                    if scan.real():
                        dve.wait_ge(s_sig, scan.count(STEPS, v + 1))
                        dve.scalar_tensor_tensor(out=gated[:, :, :], in0=s_gate[:, :, :], scalar=1.0,
                                                 in1=z[:, scan.ring, :, v, :], op0=ALU.add, op1=ALU.mult)\
                           .then_inc(s_gated, 1)
                        dve.wait_ge(s_gated, scan.count(STEPS, v + 1))
                        dve.wait_ge(leaked_ready, scan.count(STEPS, v + 1))
                        dve.scalar_tensor_tensor(out=s_pre[:, :, :], in0=gated[:, :, :], scalar=0.5,
                                                 in1=leaked[:, :, :], op0=ALU.mult, op1=ALU.add)\
                           .then_inc(s_pre_done, 1)

            rounds(dve, round_)

        @block.tensor
        def _(pe):
            mm = pe.matmul

            pe.wait_ge(consts, 2)
            pe.wait_ge(w_gate, W_GATE)
            for k in range(KD):
                ins = pe.transpose(tok_ps[:, B * k:B * (k + 1)], cond_sb[:, P * k:P * (k + 1)], ident[0:B, 0:B])
            ins = pe.transpose(tok_ps[:, HB:HB + 3 * KD], vec_rows[:, :], ident[0:3 * KD, 0:3 * KD])
            ins.then_inc(ps_ready, 1)
            for w, ps in ((gateW1, up_ps[0]), (gateW2, up_ps[1])):
                for k in range(KD):
                    for o in range(KD):
                        ins = pe.transpose(ps[:, KD * k + o, :], w[:, o, P * k:P * (k + 1)], ident[:, :])
            ins.then_inc(ps_ready, 1)
            pe.wait_ge(gate_chain, GC_COND)
            for k in range(KD):
                mm(tok_ps[:, 128:128 + E], cond_tok[:, k].rearrange("p t b -> p (t b)"), routerW[:, KD + k, :],
                   start=(k == 0), stop=(k == KD - 1))
            for n, w, src in ((0, gateW1T, condT), (1, gateW2T, hid_gate)):
                if n == 1:
                    pe.wait_ge(gate_chain, GC_HID)
                for o in range(KD):
                    for k in range(KD):
                        at = 32 + HB * n + B * o
                        ins = mm(tok_ps[:, at:at + B], w[:, k, P * o:P * (o + 1)], src[:, k, :],
                                 start=(k == 0), stop=(k == KD - 1))
                ins.then_inc(ps_ready, 1)

            def turn_leak():
                pe.wait_ge(w_leak, 16)
                pe.wait_ge(logits_ready, 2)
                for part in range(2):
                    for k in range(KD):
                        for o in range(KD):
                            at = D * part + P * k
                            ins = pe.transpose(leak_ps[:, 4 * part + KD * k + o, :], leakW[:, o, at:at + P],
                                               ident[:, :])
                ins.then_inc(ps_ready, 1)

            def add(to, w, a, start=False):
                return mm(to, w, a, start=start, stop=True, skip_group_check=True)

            def add_split(to, W, a, start=False):
                add(to, W[0], a[0], start=start)
                add(to, W[1], a[0])
                return add(to, W[0], a[1])

            def gate_inputs(c, u):
                turned, stored = c + 2, c + -3
                if u == HALVES_AT.index(1):
                    if c.i is None and c.c == 0:
                        pe.wait_ge(bias_chain, BIAS_STEPS)
                        pe.wait_ge(pick_tok_ready, 1)
                        pe.wait_ge(w_low, split_count("Wx_3"))
                    pe.wait_ge(x2_low, c.count(1, 1))
                ps = gates_ps[c.ring]
                for half in range(sum(HALVES_AT[:u]), sum(HALVES_AT[:u + 1])):
                    j, k = half // 2, half % 2
                    tile = slice(P * j, P * (j + 1))
                    if half == GATES and turned.real():
                        pe.wait_ge(logits_ready, turned.count(1, 1))
                    if half == GATES and stored.real():
                        pe.wait_ge(y_out_ready, stored.count(1, 1))
                    if k == 0:
                        add(ps[:, j, :], bias_parts[:, :], pick_tok[:, j], start=(j % 4 == 0))
                    add_split(ps[:, j, :], [w[:, k, tile] for w in Wx_p], [x[:, k] for x in x2_p])

            def scan_inputs(c, half):
                if c.i is None and c.c == 0:
                    pe.wait_ge(w_low, len(SPLITS))
                pe.wait_ge(z_split, c.count(2, half + 1))
                wait(pe, s_sig, c.count(STEPS, PART * half))
                toks = slice(PTOK * half, PTOK * (half + 1))
                for o in range(KD):
                    tile = slice(P * o, P * (o + 1))
                    add(scan_ps[:, o, toks], bias_parts[:, :], pick_tok[:, GATES + o, toks], start=(o == 0))
                    for k in range(KD):
                        add_split(scan_ps[:, o, toks], [w[:, k, tile] for w in Wz_p], [x[:, k, toks] for x in z_p])

            def recurrent(tiles, W, hi, lo, hi_ready, lo_ready, count, done):
                W_hi, W_lo = W
                pe.wait_ge(hi_ready, count)
                for j, sums in enumerate(tiles):
                    for k in range(KD):
                        add(sums, W_hi[:, k, P * j:P * (j + 1)], hi[:, k, :])
                        add(sums, W_lo[:, k, P * j:P * (j + 1)], hi[:, k, :])
                pe.wait_ge(lo_ready, count)
                for j, sums in enumerate(tiles):
                    for k in range(KD):
                        ins = add(sums, W_hi[:, k, P * j:P * (j + 1)], lo[:, k, :])
                ins.then_inc(done, 1)

            def up(c, q, part):
                ps = up_ps[q % 2]
                if part == 0:
                    if q == 0:
                        pe.wait_ge(x1_low, c.count(1, 1))
                    wait_hid(pe, c, q - 2)
                    if c.i is None and c.c == 0:
                        pe.wait_ge(w_low, split_count("w3" if q < SHARED else f"W1e_{q - SHARED}"))
                for k in range(KD):
                    if q < SHARED:
                        at = 2 * P * q + P * (part % 2)
                        W = [w[:, k, at:at + P] for w in (w1_p, w3_p)[part // 2]]
                    else:
                        W = [w[:, KD * (q - SHARED) + k, P * part:P * (part + 1)] for w in W1e_p]
                    ins = add_split(ps[:, part, :], W, [x[:, c.ring, k] for x in x1_p], start=(part == 0 and k == 0))
                if part == (3 if q < SHARED else 1):
                    ins.then_inc(up_done, 1)

            def down(c, q, part):
                if part == 0:
                    wait_hid(pe, c, q)
                    wait(pe, sum_done, c.count(UNITS, q))
                    if c.i is None and c.c == 0:
                        pe.wait_ge(w_low, split_count("w2" if q < SHARED else f"W2e_{q - SHARED}"))
                W = [w[:, 2 * q + part, :] for w in w2_p] if q < SHARED else \
                    [w[:, 2 * (q - SHARED) + part, :] for w in W2e_p]
                ins = add_split(tok_ps[:, 0:D], [h[:, q % 2, TOK * part:TOK * (part + 1)] for h in hid_p], W,
                                start=(part == 0))
                if part == 1:
                    ins.then_inc(down_done, 1)

            def piece(c, u, n):
                if c.real() and n < PIECES_AT[u]:
                    kind, q, part = PIECES[sum(PIECES_AT[:u]) + n]
                    (up if kind == "up" else down)(c, q, part)

            def round_(k):
                lstm, moe, fin, done, pre = k, k + 2, k + 1, k + -2, k + 3
                spare = gates_ps[fin.ring]
                for u in range(STEPS):
                    scan, v = scan_at(k, u)
                    if u == 0 and k.i is None and k.c == 0:
                        pe.wait_ge(w_low, split_count("Wh_3"))
                    if lstm.real():
                        recurrent([gates_ps[lstm.ring][:, j, u * B:(u + 1) * B] for j in range(GATES)], Wh_p,
                                  h_hi[:, u % 2], h_lo[:, u % 2], hi_ready, lo_ready,
                                  lstm.count(STEPS, u + 1), gates_done)
                    part, half = part_at(k, u, LAG - PART)
                    if part.real():
                        scan_inputs(part, half)
                    if scan.real():
                        recurrent([scan_ps[:, j, v * B:(v + 1) * B] for j in range(KD)], Ws_p, s_hi[:, v % 2],
                                  s_lo[:, v % 2], s_hi_ready, s_lo_ready, scan.count(STEPS, v + 1), s_done)
                    if u == SUM_TURN and fin.real():
                        pe.wait_ge(sum_done, fin.count(UNITS, UNITS))
                        for h in range(KD):
                            ins = pe.transpose(spare[:, h, :], moe_sum[:, P * h:P * (h + 1)], ident[:, :])
                        ins.then_inc(sum_turned, 1)
                    if u == X_TURN and pre.real():
                        pe.wait_ge(x_here[pre.ring], pre.pairs(16, 16))
                        for h in range(KD):
                            ins = pe.transpose(spare[:, 4 + h, :], x_in[:, pre.ring, P * h:P * (h + 1)], ident[:, :])
                        ins.then_inc(x_turned, 1)
                    if u == ROUTER and pre.real():
                        pe.wait_ge(x1_low, pre.count(1, 1))
                        if k.i is None and pre.c == 0:
                            pe.wait_ge(w_low, split_count("router"))
                        for h in range(KD):
                            for x_part, w_part in ((0, 0), (0, 1), (1, 0)):
                                ins = add(spare[:, 4, 0:E], x1_p[x_part][:, pre.ring, h], router_p[w_part][:, h],
                                          start=(h == 0 and x_part == w_part))
                        ins.then_inc(router_done, 1)
                    if u == Y_TURN and done.real():
                        pe.wait_ge(y_ready, done.count(KD, KD))
                        if pre.real():
                            pe.wait_ge(logits_ready, pre.count(1, 1))
                        for h in range(KD):
                            ins = pe.transpose(spare[:, 6 + h, :], y[:, h].rearrange("p b t -> p (b t)"), ident[:, :])
                        ins.then_inc(y_turned, 1)
                    if fin.real():
                        gate_inputs(fin, u)
                    for n in range(PIECES_AT[u]):
                        piece(moe, u, n)
                if k.i is None and k.c == -2:
                    turn_leak()

            rounds(pe, round_)


PR_COND, PR_TURNED, PR_GATE, PR_LEAK = 1, 2, (3, 4), 5
CONSTS = 6
CH_STATE = 6
GC_COND = 2 + KD
GC_PRE = (GC_COND + KD, GC_COND + KD + 2 + KD)
BIAS_STEPS = 10
GC_HID = GC_COND + KD + 2

_NAMES = ["x", "cond_1024", "L0_cond_W1", "L0_cond_b1", "L0_cond_W2", "L0_cond_b2", "L1_cond_router_W",
          "L1_cond_router_bias", "L1_cond_w1", "L1_cond_w3", "L1_cond_w2", "L1_cond_W1e", "L1_cond_W2e",
          "L2_cond_Wx", "L2_cond_Wh", "L2_cond_b", "L3_cond_W", "L3_cond_b", "L3_cond_alpha"]


def kernel(**inputs):
    import concourse.bacc as bacc
    from concourse.bass_utils import run_bass_kernel_spmd

    nc = bacc.Bacc("TRN2", target_bir_lowering=False, num_devices=1)
    arrays, args = {}, []
    for name in _NAMES:
        a = np.ascontiguousarray(inputs[name])
        arrays[name + "_dram"] = a
        args.append(nc.dram_tensor(name + "_dram", a.shape, mybir.dt.from_np(a.dtype), kind="ExternalInput").ap())
    out = nc.dram_tensor("out_dram", (B, T, D), F32, kind="ExternalOutput").ap()
    build(nc, *args, out)
    return run_bass_kernel_spmd(nc, [arrays], core_ids=[0]).results[0]["out_dram"]
```
